# Optimizing a Trainium2 kernel written in Bass

```python
import numpy as np
import jax
import jax.numpy as jnp

def _softmax(x, axis=-1):
    return jax.nn.softmax(x, axis=axis)

def _gelu(x):
    return jax.nn.gelu(x, approximate=True)

def _silu(x):
    return jax.nn.silu(x)

def _sigmoid(x):
    return jax.nn.sigmoid(x)

def _layernorm(x, axis=-1, eps=1e-05):
    m = jnp.mean(x, axis=axis, keepdims=True)
    v = jnp.var(x, axis=axis, keepdims=True)
    return (x - m) / jnp.sqrt(v + eps)

def _scatter_add(tgt, idx, src, axis=0):
    return tgt.at[idx].add(src)

def _segment_sum(src, seg, n):
    return jax.ops.segment_sum(src, seg, n)
kernel_name = 'mk_recurrent_d2_jaxref_r8_4c1522'

def setup_inputs(seed: int=0):
    np.random.seed(seed)
    _w = jnp.asarray

    def _L0_attn_setup():
        import math
        import jax, jax.numpy as jnp
        import numpy as np
        H, G = (16, 4)

        def alibi_bias(S, n_heads, dtype):
            n = 2 ** int(math.floor(math.log2(n_heads)))
            m0 = 2.0 ** (-8.0 / n)
            slopes = m0 ** np.arange(1, n + 1)
            if n < n_heads:
                m1 = 2.0 ** (-4.0 / n)
                slopes = np.concatenate([slopes, m1 ** np.arange(1, 1 + 2 * (n_heads - n), 2)])
            i = jnp.arange(S)[:, None]
            j = jnp.arange(S)[None, :]
            dist = jnp.sqrt(jnp.maximum(i - j, 0).astype(dtype))
            bias = -jnp.asarray(slopes, dtype)[:, None, None] * dist[None]
            return jnp.where((j <= i)[None], bias, jnp.asarray(-jnp.inf, dtype))
        key = jax.random.key(seed)
        ks = jax.random.split(key, 5)
        B, S, Hd = (2, 256, 256)
        D = Hd // H
        return {'x': jax.random.normal(ks[0], (B, S, Hd), jnp.float32), 'Wq': jax.random.normal(ks[1], (Hd, Hd), jnp.float32) * 0.02, 'Wk': jax.random.normal(ks[2], (G * D, Hd), jnp.float32) * 0.02, 'Wv': jax.random.normal(ks[3], (G * D, Hd), jnp.float32) * 0.02, 'Wo': jax.random.normal(ks[4], (Hd, Hd), jnp.float32) * 0.02}
    _L0_attn_in = _L0_attn_setup()

    def _L0_ffn_setup():
        import jax, jax.numpy as jnp
        import numpy as np
        B, S, D, H = (4, 256, 256, 1024)

        def fwht(x):
            orig_shape = x.shape
            n = orig_shape[-1]
            x = x.reshape(-1, n)
            h = 1
            while h < n:
                xb = x.reshape(-1, n // (2 * h), 2, h)
                a = xb[:, :, 0, :]
                b = xb[:, :, 1, :]
                x = jnp.stack([a + b, a - b], axis=2).reshape(-1, n)
                h *= 2
            scale = jnp.asarray(1.0 / np.sqrt(n), dtype=x.dtype)
            return (x * scale).reshape(orig_shape)
        key = jax.random.key(seed)
        kx, k1, k2, k3 = jax.random.split(key, 4)
        x = jax.random.normal(kx, (B, S, D), dtype=jnp.float32)
        W1 = jax.random.normal(k1, (H, D), dtype=jnp.float32) * (1.0 / np.sqrt(D))
        W2 = jax.random.normal(k2, (D, H), dtype=jnp.float32) * (1.0 / np.sqrt(H))
        W3 = jax.random.normal(k3, (H, D), dtype=jnp.float32) * (1.0 / np.sqrt(D))
        return {'x': x, 'W1': W1, 'W2': W2, 'W3': W3}
    _L0_ffn_in = _L0_ffn_setup()

    def _L1_attn_setup():
        import jax, jax.numpy as jnp
        import numpy as np
        import math
        EMBED_DIM = 256
        NUM_HEADS = 16
        DEPTH = 12
        HEAD_DIM = EMBED_DIM // NUM_HEADS // 2
        LAMBDA_INIT = 0.8 - 0.6 * math.exp(-0.3 * DEPTH)

        def _diff_attn(query, Wq, Wk, Wv, Wo, lq1, lk1, lq2, lk2, g):
            B, T, E = query.shape
            H, D = (NUM_HEADS, HEAD_DIM)
            S = T
            scaling = D ** (-0.5)
            q = (query @ Wq.T).reshape(B, T, 2 * H, D).transpose(0, 2, 1, 3)
            k = (query @ Wk.T).reshape(B, S, 2 * H, D).transpose(0, 2, 1, 3)
            v = (query @ Wv.T).reshape(B, S, H, 2 * D).transpose(0, 2, 1, 3)
            q = q * scaling
            attn = jnp.einsum('bhtd,bhsd->bhts', q, k)
            attn = jnp.nan_to_num(attn)
            causal = jnp.triu(jnp.full((T, S), -jnp.inf, attn.dtype), k=1)
            attn = jax.nn.softmax(attn + causal, axis=-1)
            lam1 = jnp.exp(jnp.sum(lq1 * lk1))
            lam2 = jnp.exp(jnp.sum(lq2 * lk2))
            lam = lam1 - lam2 + LAMBDA_INIT
            attn = attn.reshape(B, H, 2, T, S)
            attn = attn[:, :, 0] - lam * attn[:, :, 1]
            out = jnp.einsum('bhts,bhsd->bhtd', attn, v)
            rms = jax.lax.rsqrt(jnp.mean(out * out, axis=-1, keepdims=True) + 1e-05)
            out = out * rms * g
            out = out * (1.0 - LAMBDA_INIT)
            out = out.transpose(0, 2, 1, 3).reshape(B, T, H * 2 * D)
            return out @ Wo.T
        key = jax.random.key(seed)
        ks = jax.random.split(key, 9)
        B, T, E = (2, 256, EMBED_DIM)
        s = 1.0 / math.sqrt(E)
        return {'query': jax.random.normal(ks[0], (B, T, E), jnp.float32), 'Wq': jax.random.normal(ks[1], (E, E), jnp.float32) * s, 'Wk': jax.random.normal(ks[2], (E, E), jnp.float32) * s, 'Wv': jax.random.normal(ks[3], (E, E), jnp.float32) * s, 'Wo': jax.random.normal(ks[4], (E, E), jnp.float32) * s, 'lambda_q1': jax.random.normal(ks[5], (HEAD_DIM,), jnp.float32) * 0.1, 'lambda_k1': jax.random.normal(ks[6], (HEAD_DIM,), jnp.float32) * 0.1, 'lambda_q2': jax.random.normal(ks[7], (HEAD_DIM,), jnp.float32) * 0.1, 'lambda_k2': jax.random.normal(ks[8], (HEAD_DIM,), jnp.float32) * 0.1, 'subln_weight': jnp.ones((2 * HEAD_DIM,), jnp.float32)}
    _L1_attn_in = _L1_attn_setup()

    def _L1_ffn_setup():
        import jax, jax.numpy as jnp
        import numpy as np
        TOPK = 2
        N_EXPERTS = 8
        ROUTE_SCALE = 1.0
        key = jax.random.key(seed)
        ks = jax.random.split(key, 7)
        B, T, C = (4, 256, 256)
        H = 176
        HS = 352
        E = N_EXPERTS
        s = 0.02
        return {'x': jax.random.normal(ks[0], (B, T, C), jnp.float32), 'gate_w': jax.random.normal(ks[1], (E, C), jnp.float32) * s, 'gate_bias': jnp.zeros((E,), jnp.float32), 'shared_gw': jax.random.normal(ks[2], (2 * HS, C), jnp.float32) * s, 'shared_dw': jax.random.normal(ks[3], (C, HS), jnp.float32) * s, 'up_w': jax.random.normal(ks[4], (E, 2 * H, C), jnp.float32) * s, 'down_w': jax.random.normal(ks[5], (E, C, H), jnp.float32) * s}
    _L1_ffn_in = _L1_ffn_setup()
    _d = {'L0_attn_x': _L0_attn_in['x'], 'L0_attn_Wq': _L0_attn_in['Wq'], 'L0_attn_Wk': _L0_attn_in['Wk'], 'L0_attn_Wv': _L0_attn_in['Wv'], 'L0_attn_Wo': _L0_attn_in['Wo'], 'L0_ffn_W1': _L0_ffn_in['W1'], 'L0_ffn_W2': _L0_ffn_in['W2'], 'L0_ffn_W3': _L0_ffn_in['W3'], 'L1_attn_Wq': _L1_attn_in['Wq'], 'L1_attn_Wk': _L1_attn_in['Wk'], 'L1_attn_Wv': _L1_attn_in['Wv'], 'L1_attn_Wo': _L1_attn_in['Wo'], 'L1_attn_lambda_q1': _L1_attn_in['lambda_q1'], 'L1_attn_lambda_k1': _L1_attn_in['lambda_k1'], 'L1_attn_lambda_q2': _L1_attn_in['lambda_q2'], 'L1_attn_lambda_k2': _L1_attn_in['lambda_k2'], 'L1_attn_subln_weight': _L1_attn_in['subln_weight'], 'L1_ffn_gate_w': _L1_ffn_in['gate_w'], 'L1_ffn_gate_bias': _L1_ffn_in['gate_bias'], 'L1_ffn_shared_gw': _L1_ffn_in['shared_gw'], 'L1_ffn_shared_dw': _L1_ffn_in['shared_dw'], 'L1_ffn_up_w': _L1_ffn_in['up_w'], 'L1_ffn_down_w': _L1_ffn_in['down_w']}
    _x0 = _d['L0_attn_x']
    _d['L0_attn_x'] = jax.random.normal(jax.random.fold_in(jax.random.key(seed), 1), (8, 512, 256), dtype=_x0.dtype)
    del _x0
    return _d

def reference(L0_attn_x, L0_attn_Wq, L0_attn_Wk, L0_attn_Wv, L0_attn_Wo, L0_ffn_W1, L0_ffn_W2, L0_ffn_W3, L1_attn_Wq, L1_attn_Wk, L1_attn_Wv, L1_attn_Wo, L1_attn_lambda_q1, L1_attn_lambda_k1, L1_attn_lambda_q2, L1_attn_lambda_k2, L1_attn_subln_weight, L1_ffn_gate_w, L1_ffn_gate_bias, L1_ffn_shared_gw, L1_ffn_shared_dw, L1_ffn_up_w, L1_ffn_down_w):

    def _L0_attn_ref(x, Wq, Wk, Wv, Wo):
        import math
        import jax, jax.numpy as jnp
        import numpy as np
        H, G = (16, 4)

        def alibi_bias(S, n_heads, dtype):
            n = 2 ** int(math.floor(math.log2(n_heads)))
            m0 = 2.0 ** (-8.0 / n)
            slopes = m0 ** np.arange(1, n + 1)
            if n < n_heads:
                m1 = 2.0 ** (-4.0 / n)
                slopes = np.concatenate([slopes, m1 ** np.arange(1, 1 + 2 * (n_heads - n), 2)])
            i = jnp.arange(S)[:, None]
            j = jnp.arange(S)[None, :]
            dist = jnp.sqrt(jnp.maximum(i - j, 0).astype(dtype))
            bias = -jnp.asarray(slopes, dtype)[:, None, None] * dist[None]
            return jnp.where((j <= i)[None], bias, jnp.asarray(-jnp.inf, dtype))
        B, S, Hd = x.shape
        D = Hd // H
        rep = H // G
        q = (x @ Wq.T).reshape(B, S, G, rep, D)
        k = (x @ Wk.T).reshape(B, S, G, D)
        v = (x @ Wv.T).reshape(B, S, G, D)
        scale = 1.0 / math.sqrt(D)
        bias = alibi_bias(S, H, x.dtype).reshape(G, rep, S, S)
        scores = jnp.einsum('bqgrd,bkgd->bgrqk', q, k) * scale + bias
        attn = jax.nn.softmax(scores, axis=-1)
        o = jnp.einsum('bgrqk,bkgd->bqgrd', attn, v).reshape(B, S, Hd)
        return o @ Wo.T

    def _L0_ffn_ref(x, W1, W2, W3):
        import jax, jax.numpy as jnp
        import numpy as np
        B, S, D, H = (4, 256, 256, 1024)

        def fwht(x):
            orig_shape = x.shape
            n = orig_shape[-1]
            x = x.reshape(-1, n)
            h = 1
            while h < n:
                xb = x.reshape(-1, n // (2 * h), 2, h)
                a = xb[:, :, 0, :]
                b = xb[:, :, 1, :]
                x = jnp.stack([a + b, a - b], axis=2).reshape(-1, n)
                h *= 2
            scale = jnp.asarray(1.0 / np.sqrt(n), dtype=x.dtype)
            return (x * scale).reshape(orig_shape)
        up_gate = jnp.einsum('bsd,hd->bsh', x, W1)
        up_lin = jnp.einsum('bsd,hd->bsh', x, W3)
        hidden = jax.nn.silu(up_gate) * up_lin
        hidden = fwht(hidden)
        out = jnp.einsum('bsh,dh->bsd', hidden, W2)
        return out

    def _L1_attn_ref(query, Wq, Wk, Wv, Wo, lambda_q1, lambda_k1, lambda_q2, lambda_k2, subln_weight):
        import jax, jax.numpy as jnp
        import numpy as np
        import math
        EMBED_DIM = 256
        NUM_HEADS = 16
        DEPTH = 12
        HEAD_DIM = EMBED_DIM // NUM_HEADS // 2
        LAMBDA_INIT = 0.8 - 0.6 * math.exp(-0.3 * DEPTH)

        def _diff_attn(query, Wq, Wk, Wv, Wo, lq1, lk1, lq2, lk2, g):
            B, T, E = query.shape
            H, D = (NUM_HEADS, HEAD_DIM)
            S = T
            scaling = D ** (-0.5)
            q = (query @ Wq.T).reshape(B, T, 2 * H, D).transpose(0, 2, 1, 3)
            k = (query @ Wk.T).reshape(B, S, 2 * H, D).transpose(0, 2, 1, 3)
            v = (query @ Wv.T).reshape(B, S, H, 2 * D).transpose(0, 2, 1, 3)
            q = q * scaling
            attn = jnp.einsum('bhtd,bhsd->bhts', q, k)
            attn = jnp.nan_to_num(attn)
            causal = jnp.triu(jnp.full((T, S), -jnp.inf, attn.dtype), k=1)
            attn = jax.nn.softmax(attn + causal, axis=-1)
            lam1 = jnp.exp(jnp.sum(lq1 * lk1))
            lam2 = jnp.exp(jnp.sum(lq2 * lk2))
            lam = lam1 - lam2 + LAMBDA_INIT
            attn = attn.reshape(B, H, 2, T, S)
            attn = attn[:, :, 0] - lam * attn[:, :, 1]
            out = jnp.einsum('bhts,bhsd->bhtd', attn, v)
            rms = jax.lax.rsqrt(jnp.mean(out * out, axis=-1, keepdims=True) + 1e-05)
            out = out * rms * g
            out = out * (1.0 - LAMBDA_INIT)
            out = out.transpose(0, 2, 1, 3).reshape(B, T, H * 2 * D)
            return out @ Wo.T
        return _diff_attn(query, Wq, Wk, Wv, Wo, lambda_q1, lambda_k1, lambda_q2, lambda_k2, subln_weight)

    def _L1_ffn_ref(x, gate_w, gate_bias, shared_gw, shared_dw, up_w, down_w):
        import jax, jax.numpy as jnp
        import numpy as np
        TOPK = 2
        N_EXPERTS = 8
        ROUTE_SCALE = 1.0
        B, T, C = x.shape
        xf = x.reshape(-1, C)
        yg = xf @ shared_gw.T
        y, g = jnp.split(yg, 2, axis=-1)
        shared = jax.nn.silu(g) * y @ shared_dw.T
        scores = jax.nn.sigmoid(xf @ gate_w.T)
        _, topk_idx = jax.lax.top_k(scores + gate_bias, TOPK)
        w = jnp.take_along_axis(scores, topk_idx, axis=-1)
        w = w / jnp.sum(w, axis=-1, keepdims=True) * ROUTE_SCALE
        out = jnp.zeros_like(xf)
        for e in range(N_EXPERTS):
            we = jnp.sum(jnp.where(topk_idx == e, w, 0.0), axis=-1)
            gu = xf @ up_w[e].T
            g_e, u_e = jnp.split(gu, 2, axis=-1)
            h = jax.nn.silu(g_e) * u_e
            out = out + h @ down_w[e].T * we[:, None]
        return (shared + out).reshape(B, T, C)
    x = L0_attn_x
    xn = _layernorm(x, axis=-1)
    s = _L0_attn_ref(xn, L0_attn_Wq, L0_attn_Wk, L0_attn_Wv, L0_attn_Wo)
    g = _silu(_L0_ffn_ref(xn, L0_ffn_W1, L0_ffn_W2, L0_ffn_W3))
    x = x + s * g
    xn = _layernorm(x, axis=-1)
    s = _L1_attn_ref(xn, L1_attn_Wq, L1_attn_Wk, L1_attn_Wv, L1_attn_Wo, L1_attn_lambda_q1, L1_attn_lambda_k1, L1_attn_lambda_q2, L1_attn_lambda_k2, L1_attn_subln_weight)
    g = _silu(_L1_ffn_ref(xn, L1_ffn_gate_w, L1_ffn_gate_bias, L1_ffn_shared_gw, L1_ffn_shared_dw, L1_ffn_up_w, L1_ffn_down_w))
    x = x + s * g
    return x

_drawn_inputs = setup_inputs


def setup_inputs(seed=0):
    import zlib

    import numpy as np

    out = dict(_drawn_inputs(seed))
    spreads = {'L1_attn_subln_weight': (1.0, 0.2), 'L1_ffn_gate_bias': (0.0, 0.1)}
    factors = {}
    for name, (base, spread) in spreads.items():
        noise = np.random.default_rng([zlib.crc32(name.encode()), seed]).standard_normal(out[name].shape)
        drawn = base * np.exp(spread * noise) if base else spread * noise
        out[name] = jnp.asarray(drawn.astype(out[name].dtype))
    for name, factor in factors.items():
        out[name] = (out[name] * factor).astype(out[name].dtype)
    return out
```

```python
import math
from contextlib import ExitStack

import concourse.bass as bass
from concourse import mybir

F32 = mybir.dt.float32
F32R = mybir.dt.float32r
BF16 = mybir.dt.bfloat16
ALU = mybir.AluOpType
ACT = mybir.ActivationFunctionType
AX = mybir.AxisListType

P = 128
T = 512
NT = T // P
C = 256
KC = C // P
B = 8
G4 = 4
UNITS = (4, 8)
U_ALL = sum(UNITS)
DH = (16, 8)
DV = 16
NV = (4, 16)
ROWS = (48, 32)
EXP_SCALE = (1.0 / math.sqrt(16), 1.0 / math.sqrt(8))
HT = (8, 14)
SHARED_T = 3
NE = 8
EH = 176
EPS = 1e-5
LAMBDA_INIT = 0.8 - 0.6 * math.exp(-0.3 * 12)
BIG = 3.0e38
QK_MAX = 1.0e18
MROW = P - 1
PACKS = 11
SCORE_PACKS = [(0, g, 1) for g in range(4)] + [(1, g, 1) for g in range(4)] + [(2, 0, 2), (2, 2, 2), (3, 0, 4)]
MAX_PACKS = [(3, g, 1) for g in range(4)] + [(2, g, 1) for g in range(4)] + [(1, 0, 2), (1, 2, 2), (0, 0, 4)]
SLOPES = [float((2.0 ** -0.5) ** (h + 1)) for h in range(16)]


def unit_layer(u):
    return 0 if u < UNITS[0] else 1


def last_of_layer(u):
    return u in (UNITS[0] - 1, U_ALL - 1)


def gated_layers_kernel(nc, x_in, w0_qk, w0_v, w0_o, w0_up, w0_down, w1_qk, w1_v, w1_o, w1_up, w1_down,
                        w1_gate, gate_bias, lambdas, subln, c_ident, c_hadamard, c_dist, c_causal, out):
    with ExitStack() as ctx:
        def sb(name, shape, dt=F32):
            return ctx.enter_context(nc.sbuf_tensor(name, shape, dt))

        def sem(name):
            s = ctx.enter_context(nc.semaphore(name))
            sems.append(s)
            return s

        sems = []
        dram = lambda name, shape: nc.dram_tensor(name, shape, F32, kind="Internal").ap()
        q_img = [dram(f"q_img{l}", [UNITS[l] * G4, ROWS[l], T]) for l in (0, 1)]
        k_img = [dram("k_img0", [4, ROWS[0], T]), dram("k_img1", [32, ROWS[1], T])]
        gate_img = nc.dram_tensor("gate_img", [NE, T], F32, kind="Internal").ap()

        wqk = [sb("wqk0", [P, KC, 320]), sb("wqk1", [P, KC, 512])]
        wv = [sb("wv0", [P, KC, 64]), sb("wv1", [P, KC, 256])]
        wo = [sb("wo0", [P, KC, C]), sb("wo1", [P, KC, C])]
        wup0 = sb("wup0", [P, HT[0], 2, KC, P])
        wdown = [sb("wdown0", [P, HT[0], C]), sb("wdown1", [P, HT[1], C])]
        wgate = sb("wgate", [P, KC, NE])
        bias_e = sb("bias_e", [P, NE])
        lam_in = sb("lam_in", [P, 4, 8])
        lam = sb("lam", [P, 8])
        gln = sb("gln", [P, DV])
        ident = sb("ident", [P, P])
        ident_bf = sb("ident_bf", [P, P], BF16)
        causal_bf = sb("causal_bf", [P, P], BF16)
        hadamard = sb("hadamard", [P, P])
        dist = sb("dist", [P, T])
        pw = sb("pw", [P, 64])
        qring = [sb("qring0", [P, 2, G4, T], F32R), sb("qring1", [P, 2, G4, T], F32R)]
        kring = [sb("kring0", [P, 2, T], F32R), sb("kring1", [P, 2, T], F32R)]
        upring = sb("upring", [P, 3, 2, KC, P])
        gring = sb("gring", [P, 2, T])
        hbuf = sb("hbuf", [P, HT[1], T])
        probs = sb("probs", [P, 2, G4, T])
        x = sb("x", [P, NT, C])
        xn = sb("xn", [P, NT, C])
        xnT = sb("xnT", [P, KC, T])
        v = [sb("v0", [P, NT, NV[0], DV + 1]), sb("v1", [P, NT, NV[1], DV + 1])]
        shared8 = sb("shared8", [P, 2048])
        estrip = shared8[:].rearrange("p (g n) -> p g n", g=G4)
        on = shared8[:].rearrange("p (t h d) -> p t h d", t=NT, h=32)
        o_sb = xn
        oT = xnT
        ot = sb("ot", [P, T])
        tb = sb("tb", [P, T])
        wb = sb("wb", [P, T])
        fo = sb("fo", [P, NT, C])
        stats = sb("stats", [P, NT, 6])
        mv = sb("mv", [P, NT, 2])
        rstd = sb("rstd", [P, NT])
        rden = sb("rden", [P, 16])
        nmax = sb("nmax", [P, 2, NT, G4])
        mneg = sb("mneg", [G4, T], F32R)
        rt = sb("rt", [P, 6, NT, NE])
        rs = sb("rs", [P, NT])
        gT = sb("gT", [NE, T])
        ssum = sb("ssum", [P, 64])
        srstd = sb("srstd", [P, 64])

        bank = [ctx.enter_context(nc.psum_tensor(f"bank{i}", [P, 512], F32)) for i in range(8)]
        MX, SC, PV, MISC, FB = bank[0:2], bank[2:4], bank[4], bank[5], bank[6:8]

        s_w = sem("weights_loaded")
        s_z = sem("zeros_ready")
        s_imgz = sem("image_padding_written")
        s_img1 = sem("image_ones_written")
        s_fw = sem("butterflies_done")
        s_had = sem("hadamard_products_ready")
        s_hade = sem("hadamard_products_copied")
        s_lam = sem("lambda_steps")
        s_lamx = sem("lambda_exps")
        s_cst = sem("constants_ready")
        s_pvz = sem("pv_bank_zeroed")
        zero_t = hbuf[:, 0:2, :]
        ones_row = hbuf[:, 2, :]
        tmp8 = hbuf[:, 4:8, :].rearrange("p a n -> p (a n)").rearrange("p (t n) -> p t n", t=HT[0])
        n_w = 18
        with nc.Block() as block:
            @block.sync
            def _(sp):
                def ld(dst, src):
                    sp.dma_start(dst, src).then_inc(s_w, 16)

                ld(wdown[0][:], w0_down)
                ld(ident[:], c_ident)
                ld(hadamard[:], c_hadamard)
                ld(dist[:], c_dist)
                ld(tb[:, 0:P], c_causal)
                ld(wqk[0][:], w0_qk)
                ld(wv[0][:], w0_v)
                ld(wo[0][:], w0_o)
                ld(wup0[:], w0_up)
                ld(wqk[1][:], w1_qk)
                ld(wv[1][:], w1_v)
                ld(wo[1][:], w1_o)
                ld(wdown[1][:], w1_down)
                ld(wgate[:], w1_gate)
                ld(bias_e[:], gate_bias.partition_broadcast(P))
                ld(lam_in[:].rearrange("p a b -> p (a b)"), lambdas.partition_broadcast(P))
                ld(gln[:], subln.partition_broadcast(P))
                sp.wait_ge(s_z, 1)
                for img in (q_img[1], k_img[1]):
                    sp.dma_start(img[:, 24:32, :], zero_t).then_inc(s_imgz, 16)
                sp.wait_ge(s_imgz, 32)
                sp.dma_start(k_img[1][3:32:4, 31, :], ones_row[0:8, :]).then_inc(s_img1, 16)
                sp.wait_ge(s_img1, 16)

            @block.vector
            def _(dve):
                nc.vector.memset(hbuf[:, 0:2, :], 0.0)
                nc.vector.memset(ones_row, 1.0).then_inc(s_z, 1)
                for l in (0, 1):
                    nc.vector.memset(qring[l][:].rearrange("p a g n -> p (a g n)").bitcast(F32), 0.0)
                    nc.vector.memset(v[l][:].rearrange("p t h d -> p (t h d)"), 1.0)
                nc.vector.memset(kring[0][:].rearrange("p a n -> p (a n)").bitcast(F32), 0.0)
                nc.vector.memset(rt[:].rearrange("p a t e -> p (a t e)"), BIG)
                nc.vector.memset(pw[:], -0.5).then_inc(s_z, 1)
                dve.wait_ge(s_w, 16 * (n_w - 1))
                nc.vector.tensor_copy(ident_bf[:], ident[:]).then_inc(s_cst, 1)
                nc.vector.tensor_copy(causal_bf[:], tb[:, 0:P]).then_inc(s_cst, 1)
                for i in (0, 1):
                    nc.vector.tensor_tensor(lam_in[:, 2 * i, :], lam_in[:, 2 * i, :], lam_in[:, 2 * i + 1, :],
                                            ALU.mult).then_inc(s_lam, 1)
                dve.wait_ge(s_lam, 2)
                nc.vector.tensor_reduce(lam[:, 0:2], lam_in[:, 0:4:2, :], AX.X, ALU.add).then_inc(s_lam, 1)
                dve.wait_ge(s_lamx, 1)
                nc.vector.tensor_tensor(lam[:, 4:5], lam[:, 3:4], lam[:, 2:3], ALU.subtract).then_inc(s_lam, 1)
                dve.wait_ge(s_lam, 4)
                nc.vector.tensor_scalar(lam[:, 5:6], lam[:, 4:5], -LAMBDA_INIT, None, ALU.add).then_inc(s_lam, 1)
                nc.vector.tensor_scalar(gln[:], gln[:], 1.0 - LAMBDA_INIT, None, ALU.mult).then_inc(s_lam, 1)
                src, dst = wdown[0][:], tmp8
                n = 0
                for b in (1, 2, 4):
                    for i in range(0, HT[0], 2 * b):
                        lo, hi = slice(i, i + b), slice(i + b, i + 2 * b)
                        nc.vector.tensor_tensor(dst[:, lo, :], src[:, lo, :], src[:, hi, :], ALU.add).then_inc(s_fw, 1)
                        nc.vector.tensor_tensor(dst[:, hi, :], src[:, lo, :], src[:, hi, :],
                                                ALU.subtract).then_inc(s_fw, 1)
                        n += 2
                    dve.wait_ge(s_fw, n)
                    src, dst = dst, src

            @block.scalar
            def _(act):
                act.wait_ge(s_lam, 3)
                nc.scalar.activation(lam[:, 2:4], lam[:, 0:2], ACT.Exp).then_inc(s_lamx, 1)
                for t in range(HT[0]):
                    act.wait_ge(s_had, t + 1)
                    nc.scalar.copy(wdown[0][:, t, :], bank[t % 4][:, 0:C]).then_inc(s_hade, 1)
                act.wait_ge(s_hade, HT[0])

            @block.tensor
            def _(pe):
                pe.wait_ge(s_fw, 14)
                for t in range(HT[0]):
                    if t >= 4:
                        pe.wait_ge(s_hade, t - 3)
                    nc.tensor.matmul(bank[t % 4][:, 0:C], hadamard[:], tmp8[:, t, :],
                                     start=True, stop=True).then_inc(s_had, 1)
                pe.wait_ge(s_z, 1)
                nc.tensor.matmul(PV[:], hbuf[:, 0, 0:P], hbuf[:, 0, :], start=True, stop=True).then_inc(s_pvz, 1)
                pe.wait_ge(s_pvz, 1)

        nc.all_engine_barrier()

        sems.clear()
        s_x = sem("x_loaded")
        s_stat = sem("stats_ready")
        s_aggr = sem("moments_ready")
        s_veps = sem("variance_plus_eps_ready")
        s_rstd = sem("rstd_ready")
        s_xn = sem("xn_ready")
        s_xnTp = sem("xnT_in_psum")
        s_xnT = sem("xnT_ready")
        s_proj = sem("projection_in_psum")
        s_pc = sem("projection_copied")
        s_phi = sem("projection_high_ready")
        s_plo = sem("projection_low_ready")
        s_img = [sem(f"image_of_projection_{i}_written") for i in range(4)]
        s_vp = sem("v_in_psum")
        s_v = sem("v_ready")
        s_rp = sem("router_logits_in_psum")
        s_rtk = sem("router_steps")
        s_rsg = sem("router_tanh_ready")
        s_rT = sem("router_weights_transposed")
        s_rTc = sem("router_weights_copied")
        s_rimg = sem("router_weights_written")
        s_ring = [sem("ring_loaded_even"), sem("ring_loaded_odd")]
        s_mp = sem("max_scores_in_psum")
        s_mr = sem("max_reduced")
        s_mT = sem("max_transposed")
        s_mc = sem("max_copied")
        s_mrow = sem("max_rows_loaded")
        s_sc = sem("scores_in_psum")
        s_exp = sem("exps_ready")
        s_es = sem("distance_factors_ready")
        s_pm = sem("probs_masked")
        s_pv = sem("pv_done")
        s_ot = sem("pv_copied")
        s_oTp = sem("outputs_transposed")
        s_rd = sem("denominators_inverted")
        s_on = sem("outputs_normalised")
        s_up = [sem("up_weights_loaded0"), sem("up_weights_loaded1"), sem("up_weights_loaded2")]
        s_gr = [sem("expert_weights_loaded_even"), sem("expert_weights_loaded_odd")]
        s_g = sem("gate_half_in_psum")
        s_u = sem("linear_half_in_psum")
        s_t = sem("tanh_ready")
        s_gu = sem("gate_half_used")
        s_h = sem("hidden_ready")
        s_hw = sem("hidden_weighted")
        s_dn = sem("down_in_psum")
        s_fo = sem("ffn_silu_ready")
        s_rm = sem("rms_steps")
        s_rmp = sem("rms_pool_steps")
        s_oTt = sem("o_transposed_in_psum")
        s_oTs = sem("oT_ready")
        s_so = sem("attention_out_in_psum")
        s_gx = sem("gated_ready")
        s_xr = sem("x_updated")
        s_out = sem("out_written")
        body_sems = list(sems)

        PT = ((0, 2, 1), (0, 2, 1, 3))
        NPT = (3, 4)
        PROJ = [
            [(True, 0, 128, 0), (False, 256, 64, 0), (True, 128, 128, 8)],
            [(True, 0, 128, 0), (False, 256, 128, 0), (True, 128, 128, 16), (False, 384, 128, 16)],
        ]
        PROJ_BANK = [SC[0], SC[1], FB[0], FB[1]]
        proj0 = (0, NPT[0])
        tile0 = (0, HT[0])
        img0 = (0, NPT[0] * 3)

        def stage(i, part):
            return hbuf[:, 3 * i + part, :]

        def wait_images(eng, l, tiles):
            for i in range(tiles):
                eng.wait_ge(s_img[i], 48 * (1 + (l == 1 and i < NPT[0])))

        def gated(l, j):
            return l == 1 and j >= SHARED_T

        def tiles_of_unit(u):
            l = unit_layer(u)
            w = u - (0, UNITS[0])[l]
            return l, (2 * w, 2 * w + 1) if 2 * w < HT[l] else None

        with nc.Fori(0, B) as b:
            with nc.Block() as block:
                @block.sync
                def _(sp):
                    def ring_load(u):
                        l = unit_layer(u)
                        w = u - (0, UNITS[0])[l]
                        s = u % 2
                        if u >= 2:
                            sp.wait_ge(s_sc, PACKS * (u - 1))
                        if l == 0:
                            wait_images(sp, 0, 2 if w < 2 else 3)
                            sp.dma_start(qring[0][0:48, s, :, :].bitcast(F32),
                                         q_img[0][4 * w:4 * w + 4].rearrange("g r n -> r g n")).then_inc(s_ring[s], 16)
                            sp.dma_start(kring[0][0:48, s, :].bitcast(F32), k_img[0][w]).then_inc(s_ring[s], 16)
                        else:
                            wait_images(sp, 1, 2 if w < 4 else 4)
                            for g in range(G4):
                                sp.dma_start(qring[1][32 * g:32 * g + 32, s, g, :].bitcast(F32),
                                             q_img[1][4 * w + g]).then_inc(s_ring[s], 16)
                            sp.dma_start(kring[1][:, s, :].bitcast(F32),
                                         k_img[1][4 * w:4 * w + 4].rearrange("g r n -> (g r) n")).then_inc(s_ring[s], 16)

                    def max_row(u):
                        sp.wait_ge(s_mc, u + 1)
                        sp.dma_start(qring[unit_layer(u)][MROW:MROW + 1, u % 2, :, :].bitcast(F32),
                                     mneg[:].bitcast(F32)).then_inc(s_mrow, 16)

                    def up_load(j):
                        if j >= 3:
                            sp.wait_ge(s_u, HT[0] + j - 2)
                        sp.dma_start(upring[:, j % 3], w1_up[j]).then_inc(s_up[j % 3], 16)

                    def gate_load(j):
                        n = j - SHARED_T
                        if n >= 2:
                            sp.wait_ge(s_hw, n - 1)
                        r = P * n
                        while r < P * n + P:
                            e = r // EH
                            m = min(EH * (e + 1), P * n + P) - r
                            sp.dma_start(gring[r - P * n:r - P * n + m, n % 2, :],
                                         gate_img[e].partition_broadcast(m)).then_inc(s_gr[n % 2], 16)
                            r += m

                    def images(l):
                        for i, (is_q, _, m, h0) in enumerate(PROJ[l]):
                            d = DH[l]
                            img = (q_img if is_q else k_img)[l][h0:h0 + m // d]
                            terms = (0, 0, 1) if is_q else (0, 1, 0)
                            sp.wait_ge(s_phi, proj0[l] + i + 1)
                            sp.wait_ge(s_plo, proj0[l] + i + 1)
                            for t, part in enumerate(terms):
                                sp.dma_start(img[:, d * t:d * t + d, :],
                                             stage(i, part)[0:m, :]).then_inc(s_img[i], 16)

                    sp.dma_start(x[:], x_in[bass.ts(b, T), :].rearrange("(t p) c -> p t c", p=P)).then_inc(s_x, 16)
                    images(0)
                    ring_load(0)
                    ring_load(1)
                    max_row(0)
                    for u in range(U_ALL):
                        l, tiles = tiles_of_unit(u)
                        if u >= 1 and not last_of_layer(u) and not last_of_layer(u - 1):
                            ring_load(u + 1)
                        if l == 1 and tiles:
                            for j in tiles:
                                if j + 2 < HT[1]:
                                    up_load(j + 2)
                                if gated(1, j):
                                    gate_load(j)
                        if not last_of_layer(u):
                            max_row(u + 1)
                        if u == UNITS[0] - 1:
                            images(1)
                            ring_load(u + 1)
                            ring_load(u + 2)
                            up_load(0)
                            up_load(1)
                            sp.wait_ge(s_rTc, 1)
                            sp.dma_start(gate_img, gT[:]).then_inc(s_rimg, 16)
                            sp.wait_ge(s_rimg, 16)
                            max_row(u + 1)
                    sp.wait_ge(s_xr, 8)
                    sp.dma_start(out[bass.ts(b, T), :].rearrange("(t p) c -> p t c", p=P), x[:]).then_inc(s_out, 16)
                    sp.wait_ge(s_out, 16)

                @block.tensor
                def _(pe):
                    def max_pack(u, i):
                        l, s = unit_layer(u), u % 2
                        n = PACKS * u + i
                        qt, g0, heads = MAX_PACKS[i]
                        w = P * (qt + 1)
                        if n >= 2:
                            pe.wait_ge(s_mr, n - 1)
                        for g in range(g0, g0 + heads):
                            o = MX[n % 2][:, (g - g0) * w:(g - g0 + 1) * w]
                            nc.tensor.matmul(o, qring[l][0:MROW, s, g, qt * P:(qt + 1) * P],
                                             kring[l][0:MROW, s, 0:w], start=True, stop=True)
                            last = nc.tensor.matmul(o[:, qt * P:], ident_bf[:], causal_bf[:], start=False, stop=True,
                                                    skip_group_check=True)
                        last.then_inc(s_mp, 1)

                    def wait_ring(u):
                        n = sum(2 if unit_layer(i) == 0 else 5 for i in range(u % 2, u + 1, 2))
                        pe.wait_ge(s_ring[u % 2], 16 * n)

                    def max_turn(u):
                        pe.wait_ge(s_mr, PACKS * (u + 1))
                        if u:
                            pe.wait_ge(s_mc, u)
                        if u >= 2:
                            pe.wait_ge(s_on, u - 1)
                        for qt in range(NT):
                            last = nc.tensor.transpose(MISC[0:G4, qt * P:(qt + 1) * P], nmax[:, u % 2, qt, :],
                                                       ident[:])
                        last.then_inc(s_mT, 1)

                    def score_pack(u, i):
                        l, s = unit_layer(u), u % 2
                        n = PACKS * u + i
                        kt, g0, heads = SCORE_PACKS[i]
                        w = T - P * kt
                        if n >= 2:
                            pe.wait_ge(s_exp, n - 1)
                        if i == 0:
                            pe.wait_ge(s_mrow, 16 * (u + 1))
                        for g in range(g0, g0 + heads):
                            last = nc.tensor.matmul(SC[n % 2][:, (g - g0) * w:(g - g0 + 1) * w],
                                                    kring[l][:, s, kt * P:(kt + 1) * P],
                                                    qring[l][:, s, g, kt * P:T], start=True, stop=True)
                        last.then_inc(s_sc, 1)

                    def pv(u, kt):
                        l = unit_layer(u)
                        pe.wait_ge(s_pm, 4 * u + kt + 1)
                        if kt == 0 and u:
                            pe.wait_ge(s_ot, u)
                        for g in range(G4):
                            hv = (u if l == 0 else 2 * (u - UNITS[0]) + g // 2)
                            last = nc.tensor.matmul(PV[32 * g:32 * g + DV + 1, kt * P:T], v[l][:, kt, hv, :],
                                                    probs[:, kt % 2, g, 0:T - P * kt], start=(kt == 0),
                                                    stop=(kt == NT - 1), skip_group_check=True)
                        last.then_inc(s_pv, 1)

                    def out_turn(u):
                        pe.wait_ge(s_ot, u + 1)
                        if not last_of_layer(u):
                            pe.wait_ge(s_mc, u + 2)
                        else:
                            pe.wait_ge(s_on, u)
                        for tt in range(NT):
                            last = nc.tensor.transpose(MISC[:, tt * P:(tt + 1) * P], ot[:, tt * P:(tt + 1) * P],
                                                       ident[:])
                        last.then_inc(s_oTp, 1)

                    def up(l, j, half):
                        n = tile0[l] + j
                        if half == 0 and n:
                            pe.wait_ge(s_gu, n)
                        if half == 1 and n:
                            pe.wait_ge(s_h, n)
                        if l == 1 and half == 0:
                            pe.wait_ge(s_up[j % 3], 16 * (j // 3 + 1))
                        for k in range(KC):
                            wt = wup0[:, j, half, k, :] if l == 0 else upring[:, j % 3, half, k, :]
                            last = nc.tensor.matmul(FB[half][:], wt, xnT[:, k, :], start=(k == 0), stop=(k == KC - 1))
                        last.then_inc((s_g, s_u)[half], 1)

                    def down(l, tt):
                        if tt == 0:
                            pe.wait_ge(s_h, tile0[l] + HT[l])
                            if l == 1:
                                pe.wait_ge(s_hw, HT[1] - SHARED_T)
                        for j in range(HT[l]):
                            last = nc.tensor.matmul(FB[tt // 2][:, (tt % 2) * C:(tt % 2 + 1) * C],
                                                    hbuf[:, j, tt * P:(tt + 1) * P], wdown[l][:, j, :],
                                                    start=(j == 0), stop=(j == HT[l] - 1))
                        if tt % 2:
                            last.then_inc(s_dn, 1)

                    def piece(u, i):
                        l, tiles = tiles_of_unit(u)
                        if tiles:
                            up(l, tiles[i // 2], i % 2)
                        else:
                            down(l, i)

                    def prologue(l):
                        pe.wait_ge(s_xn, l + 1)
                        for k in range(KC):
                            for tt in range(NT):
                                last = nc.tensor.transpose(FB[k][:, tt * P:(tt + 1) * P], xn[:, tt, k * P:(k + 1) * P],
                                                           ident[:])
                            last.then_inc(s_xnTp, 1)
                        pe.wait_ge(s_xnT, 2 * (l + 1))
                        for i, (_, c0, m, _) in enumerate(PROJ[l]):
                            for k in range(KC):
                                last = nc.tensor.matmul(PROJ_BANK[i][0:m, :], wqk[l][:, k, c0:c0 + m], xnT[:, k, :],
                                                        start=(k == 0), stop=(k == KC - 1))
                            last.then_inc(s_proj, 1)
                        w = DV * NV[l]
                        for tt in range(NT):
                            vb = MX[0][:, tt * w:(tt + 1) * w] if l == 0 else MX[tt // 2][:, (tt % 2) * w:(tt % 2 + 1) * w]
                            for k in range(KC):
                                last = nc.tensor.matmul(vb, xnT[:, k, tt * P:(tt + 1) * P], wv[l][:, k, :],
                                                        start=(k == 0), stop=(k == KC - 1))
                        last.then_inc(s_vp, 1)
                        if l == 1:
                            for tt in range(NT):
                                for k in range(KC):
                                    last = nc.tensor.matmul(MISC[:, tt * NE:(tt + 1) * NE],
                                                            xnT[:, k, tt * P:(tt + 1) * P], wgate[:, k, :],
                                                            start=(k == 0), stop=(k == KC - 1))
                            last.then_inc(s_rp, 1)
                            pe.wait_ge(s_rtk, 9)
                            for tt in range(NT):
                                last = nc.tensor.transpose(MISC[0:NE, tt * P:(tt + 1) * P], rt[:, 4, tt, :], ident[:])
                            last.then_inc(s_rT, 1)
                        u = (0, UNITS[0])[l]
                        pe.wait_ge(s_v, l + 1)
                        wait_ring(u)
                        for i in range(PACKS):
                            max_pack(u, i)
                        if l == 1:
                            pe.wait_ge(s_rTc, 1)
                        max_turn(u)
                        pe.wait_ge(s_pc, proj0[l] + NPT[l])

                    def epilogue(l):
                        if l == 0:
                            for tt in range(NT):
                                down(0, tt)
                        pe.wait_ge(s_on, UNITS[0] if l == 0 else U_ALL)
                        if l == 1:
                            pe.wait_ge(s_rm, 5)
                        for k in range(KC):
                            for tt in range(NT):
                                last = nc.tensor.transpose(MX[k][:, tt * P:(tt + 1) * P],
                                                           o_sb[:, tt, k * P:(k + 1) * P], ident[:])
                            last.then_inc(s_oTt, 1)
                        pe.wait_ge(s_oTs, 2 * (l + 1))
                        for tt in range(NT):
                            for k in range(KC):
                                last = nc.tensor.matmul(SC[tt // 2][:, (tt % 2) * C:(tt % 2 + 1) * C],
                                                        oT[:, k, tt * P:(tt + 1) * P], wo[l][:, k, :],
                                                        start=(k == 0), stop=(k == KC - 1))
                            if tt % 2:
                                last.then_inc(s_so, 1)

                    for l in (0, 1):
                        prologue(l)
                        for u in range((0, UNITS[0])[l], (UNITS[0], U_ALL)[l]):
                            more = not last_of_layer(u)
                            if more:
                                wait_ring(u + 1)
                            for i in range(PACKS):
                                score_pack(u, i)
                                if more:
                                    max_pack(u + 1, i)
                                if i == 3:
                                    piece(u, 0)
                                if i == 5:
                                    pv(u, 0)
                                if i == 7:
                                    piece(u, 1)
                                if i == 8:
                                    pv(u, 1)
                            pv(u, 2)
                            piece(u, 2)
                            pv(u, 3)
                            if more:
                                max_turn(u + 1)
                            piece(u, 3)
                            out_turn(u)
                        epilogue(l)

                @block.scalar
                def _(act):
                    def exps(u, i):
                        l = unit_layer(u)
                        n = PACKS * u + i
                        kt, g0, heads = SCORE_PACKS[i]
                        w = T - P * kt
                        act.wait_ge(s_sc, n + 1)
                        if 4 * u + kt >= 2:
                            act.wait_ge(s_pv, 4 * u + kt - 1)
                        nc.scalar.activation(probs[:, kt % 2, g0:g0 + heads, 0:w],
                                             SC[n % 2][:, 0:heads * w].rearrange("p (g n) -> p g n", g=heads),
                                             ACT.Exp, scale=EXP_SCALE[l]).then_inc(s_exp, 1)

                    def strips(u):
                        if u:
                            act.wait_ge(s_pm, 4 * u)
                        for g in range(G4):
                            nc.scalar.activation(estrip[:, g, :], dist[:], ACT.Exp,
                                                 scale=-SLOPES[4 * u + g]).then_inc(s_es, 1)

                    def max_copy(u):
                        act.wait_ge(s_mT, u + 1)
                        if u:
                            act.wait_ge(s_mrow, 16 * u)
                        nc.scalar.copy(mneg[:], MISC[0:G4, :]).then_inc(s_mc, 1)

                    def tanh_tile(u, i):
                        l, tiles = tiles_of_unit(u)
                        if tiles:
                            n = tile0[l] + tiles[i]
                            act.wait_ge(s_g, n + 1)
                            if n:
                                act.wait_ge(s_gu, n)
                            if n == tile0[1]:
                                act.wait_ge(s_fo, 2)
                            nc.scalar.activation(tb[:], FB[0][:], ACT.Tanh, scale=0.5).then_inc(s_t, 1)
                        else:
                            tanh_down(l, i)

                    def tanh_down(l, i):
                        act.wait_ge(s_dn, 2 * l + i + 1)
                        act.wait_ge(s_gu, tile0[l] + HT[l])
                        if i:
                            act.wait_ge(s_fo, 2 * l + i)
                        nc.scalar.activation(tb[:], FB[i][:], ACT.Tanh, scale=0.5).then_inc(s_t, 1)

                    def prologue(l):
                        for k in range(KC):
                            act.wait_ge(s_xnTp, 2 * l + k + 1)
                            nc.scalar.copy(xnT[:, k, :], FB[k][:]).then_inc(s_xnT, 1)
                        for i, (_, _, m, _) in enumerate(PROJ[l]):
                            act.wait_ge(s_pc, proj0[l] + i + 1)
                            nc.scalar.copy(stage(i, 0)[0:m, :].bitcast(F32R), stage(i, 2)[0:m, :]).then_inc(s_phi, 1)
                        act.wait_ge(s_vp, l + 1)
                        if l == 0:
                            nc.scalar.copy(v[0][:, :, :, 0:DV],
                                           MX[0][:, 0:256].rearrange("p (t h d) -> p t h d", t=NT, h=4)).then_inc(s_v, 1)
                        else:
                            for i in range(2):
                                last = nc.scalar.copy(v[1][:, 2 * i:2 * i + 2, :, 0:DV],
                                                      MX[i][:].rearrange("p (t h d) -> p t h d", t=2, h=16))
                            last.then_inc(s_v, 1)
                            act.wait_ge(s_rp, 1)
                            nc.scalar.activation(rt[:, 0].rearrange("p t e -> p (t e)"), MISC[:, 0:NT * NE], ACT.Tanh,
                                                 scale=0.5).then_inc(s_rsg, 1)
                            act.wait_ge(s_rT, 1)
                            nc.scalar.copy(gT[:], MISC[0:NE, :]).then_inc(s_rTc, 1)
                        if l == 0:
                            strips(0)
                        max_copy((0, UNITS[0])[l])

                    for l in (0, 1):
                        prologue(l)
                        for u in range((0, UNITS[0])[l], (UNITS[0], U_ALL)[l]):
                            for i in range(PACKS):
                                exps(u, i)
                                if i == 6:
                                    tanh_tile(u, 0) if tiles_of_unit(u)[1] else None
                            if not tiles_of_unit(u)[1]:
                                tanh_down(l, 0)
                            else:
                                tanh_tile(u, 1)
                            act.wait_ge(s_pv, 4 * (u + 1))
                            if u:
                                act.wait_ge(s_oTp, u)
                            nc.scalar.copy(ot[:], PV[:]).then_inc(s_ot, 1)
                            if not last_of_layer(u):
                                max_copy(u + 1)
                                if l == 0:
                                    strips(u + 1)
                            if not tiles_of_unit(u)[1]:
                                tanh_down(l, 1)
                        if l == 0:
                            tanh_down(0, 0)
                            tanh_down(0, 1)
                        for k in range(KC):
                            act.wait_ge(s_oTt, 2 * l + k + 1)
                            nc.scalar.copy(oT[:, k, :], MX[k][:]).then_inc(s_oTs, 1)

                @block.vector
                def _(dve):
                    def layernorm(l):
                        for tt in range(NT):
                            nc.vector.bn_stats(stats[:, tt, :], x[:, tt, :]).then_inc(s_stat, 1)
                        dve.wait_ge(s_stat, NT * (l + 1))
                        for tt in range(NT):
                            nc.vector.bn_aggr(mv[:, tt, :], stats[:, tt, :]).then_inc(s_aggr, 1)
                        dve.wait_ge(s_rstd, l + 1)
                        for tt in range(NT):
                            last = nc.vector.tensor_scalar(xn[:, tt, :], x[:, tt, :], mv[:, tt, 0:1],
                                                           rstd[:, tt:tt + 1], ALU.subtract, ALU.mult)
                        last.then_inc(s_xn, 1)

                    def maxima(u, i):
                        qt, g0, heads = MAX_PACKS[i]
                        w = P * (qt + 1)
                        n = PACKS * u + i
                        dve.wait_ge(s_mp, n + 1)
                        if i == 0 and u >= 2:
                            dve.wait_ge(s_mT, u - 1)
                        nc.vector.tensor_reduce(nmax[:, u % 2, qt, g0:g0 + heads],
                                                MX[n % 2][:, 0:heads * w].rearrange("p (g n) -> p g n", g=heads),
                                                AX.X, ALU.max, negate=True).then_inc(s_mr, 1)

                    def distances(u, kt):
                        w = T - P * kt
                        dve.wait_ge(s_exp, PACKS * u + (4, 8, 10, 11)[kt])
                        dve.wait_ge(s_es, G4 * (u + 1))
                        pr = probs[:, kt % 2, :, 0:w]
                        nc.vector.scalar_tensor_tensor(pr, pr, BIG, estrip[:, :, 0:w], ALU.min,
                                                       ALU.mult).then_inc(s_pm, 1)

                    def gate_half(l, j):
                        n = tile0[l] + j
                        dve.wait_ge(s_t, n + 1 + (2 if l else 0))
                        if n:
                            dve.wait_ge(s_h, n)
                        nc.vector.scalar_tensor_tensor(wb[:], tb[:], 1.0, FB[0][:], ALU.add, ALU.mult).then_inc(s_gu, 1)

                    def linear_half(l, j):
                        n = tile0[l] + j
                        dve.wait_ge(s_u, n + 1)
                        dve.wait_ge(s_gu, n + 1)
                        if j < 12:
                            wait_images(dve, l, NPT[l])
                        nc.vector.scalar_tensor_tensor(hbuf[:, j, :], wb[:], 0.5, FB[1][:], ALU.mult,
                                                       ALU.mult).then_inc(s_h, 1)

                    def down_half(l, i):
                        dve.wait_ge(s_t, (HT[0] if l == 0 else HT[0] + 2 + HT[1]) + i + 1)
                        nc.vector.scalar_tensor_tensor(fo[:, 2 * i:2 * i + 2, :].rearrange("p t c -> p (t c)"), tb[:], 1.0,
                                                       FB[i][:], ALU.add, ALU.mult).then_inc(s_fo, 1)

                    def normalise(u):
                        l = unit_layer(u)
                        dve.wait_ge(s_oTp, u + 1)
                        m = MISC[:].rearrange("p (a c) -> p a c", c=32)
                        if u:
                            dve.wait_ge(s_on, u)
                        nc.vector.reciprocal(rden[:], m[:, :, DV]).then_inc(s_rd, 1)
                        dve.wait_ge(s_rd, u + 1)
                        if l == 0:
                            o = o_sb[:, :, 64 * u:64 * u + 64].rearrange("p t (g d) -> p t g d", g=G4)
                        else:
                            w = u - UNITS[0]
                            o = on[:, :, 4 * w:4 * w + 4, :]
                        nc.vector.tensor_tensor(
                            o, MISC[:].rearrange("p (t g c) -> p t g c", t=NT, g=G4)[:, :, :, 0:DV],
                            rden[:].rearrange("p (t g) -> p t g", t=NT).unsqueeze(3).to_broadcast([P, NT, G4, DV]),
                            ALU.mult).then_inc(s_on, 1)

                    def router():
                        sc, sb_, top, two, w, rep = (rt[:, i] for i in range(6))
                        dve.wait_ge(s_rsg, 1)
                        nc.vector.tensor_scalar(sc, sc, 1.0, 0.5, ALU.add, ALU.mult).then_inc(s_rtk, 1)
                        dve.wait_ge(s_rtk, 1)
                        nc.vector.tensor_tensor(sb_, sc, bias_e[:].unsqueeze(1).to_broadcast([P, NT, NE]),
                                                ALU.add).then_inc(s_rtk, 1)
                        dve.wait_ge(s_rtk, 2)
                        for tt in range(NT):
                            last = nc.vector.max(top[:, tt, :], sb_[:, tt, :])
                        last.then_inc(s_rtk, 1)
                        dve.wait_ge(s_rtk, 3)
                        nc.vector.tensor_copy(two[:, :, 0:2], top[:, :, 0:2]).then_inc(s_rtk, 1)
                        dve.wait_ge(s_rtk, 4)
                        for tt in range(NT):
                            last = nc.vector.match_replace(rep[:, tt, :], two[:, tt, :], sb_[:, tt, :], -BIG)
                        last.then_inc(s_rtk, 1)
                        dve.wait_ge(s_rtk, 5)
                        nc.vector.scalar_tensor_tensor(w, rep, -BIG, sc, ALU.is_equal, ALU.mult).then_inc(s_rtk, 1)
                        dve.wait_ge(s_rtk, 6)
                        nc.vector.tensor_reduce(rs[:], w, AX.X, ALU.add).then_inc(s_rtk, 1)
                        dve.wait_ge(s_rtk, 7)
                        nc.vector.reciprocal(rs[:], rs[:]).then_inc(s_rtk, 1)
                        dve.wait_ge(s_rtk, 8)
                        nc.vector.tensor_tensor(w, w, rs[:].unsqueeze(2).to_broadcast([P, NT, NE]),
                                                ALU.mult).then_inc(s_rtk, 1)

                    def rms():
                        pair = on.rearrange("p t (h two) d -> p (t h) two d", two=2)
                        o3 = o_sb[:].rearrange("p t (h d) -> p (t h) d", d=DV)
                        sq = hbuf[:, 0:2, :].rearrange("p a n -> p (a n)").rearrange("p (h d) -> p h d", d=DV)
                        dve.wait_ge(s_on, U_ALL)
                        nc.vector.scalar_tensor_tensor(o3, pair[:, :, 1, :], lam[:, 5:6], pair[:, :, 0, :], ALU.mult,
                                                       ALU.add).then_inc(s_rm, 1)
                        dve.wait_ge(s_rm, 1)
                        dve.wait_ge(s_dn, 4)
                        nc.vector.tensor_tensor(sq, o3, o3, ALU.mult).then_inc(s_rm, 1)
                        dve.wait_ge(s_rm, 2)
                        nc.vector.tensor_reduce(ssum[:], sq, AX.X, ALU.add).then_inc(s_rm, 1)
                        dve.wait_ge(s_rmp, 2)
                        nc.vector.tensor_tensor(o3, o3, srstd[:].unsqueeze(2).to_broadcast([P, 64, DV]),
                                                ALU.mult).then_inc(s_rm, 1)
                        dve.wait_ge(s_rm, 4)
                        nc.vector.tensor_tensor(o3, o3, gln[:].unsqueeze(1).to_broadcast([P, 64, DV]),
                                                ALU.mult).then_inc(s_rm, 1)

                    def update_x(l):
                        for i in range(2):
                            dve.wait_ge(s_so, 2 * l + i + 1)
                            dve.wait_ge(s_fo, 2 * l + i + 1)
                            f = fo[:, 2 * i:2 * i + 2, :].rearrange("p t c -> p (t c)")
                            nc.vector.scalar_tensor_tensor(f, SC[i][:], 0.5, f, ALU.mult, ALU.mult).then_inc(s_gx, 1)
                            dve.wait_ge(s_gx, 2 * l + i + 1)
                            for tt in (2 * i, 2 * i + 1):
                                nc.vector.tensor_tensor(x[:, tt, :], x[:, tt, :], fo[:, tt, :],
                                                        ALU.add).then_inc(s_xr, 1)

                    dve.wait_ge(s_x, 16)
                    for l in (0, 1):
                        if l:
                            dve.wait_ge(s_xr, 4)
                        layernorm(l)
                        for i, (_, _, m, _) in enumerate(PROJ[l]):
                            dve.wait_ge(s_proj, proj0[l] + i + 1)
                            if l == 1:
                                nc.vector.tensor_scalar(stage(i, 2)[0:m, :], PROJ_BANK[i][0:m, :], QK_MAX, -QK_MAX,
                                                        ALU.min, ALU.max).then_inc(s_pc, 1)
                            else:
                                nc.vector.tensor_copy(stage(i, 2)[0:m, :], PROJ_BANK[i][0:m, :]).then_inc(s_pc, 1)
                        if l == 1:
                            router()
                        u0 = (0, UNITS[0])[l]
                        for i in range(PACKS):
                            maxima(u0, i)
                        for u in range(u0, u0 + UNITS[l]):
                            _, tiles = tiles_of_unit(u)
                            more = not last_of_layer(u)
                            for i in range(PACKS):
                                if more:
                                    maxima(u + 1, i)
                                if l == 0 and i in (3, 7, 9):
                                    distances(u, (3, 7, 9).index(i))
                                if i == 6 and tiles:
                                    gate_half(l, tiles[0])
                                if i == 8 and tiles:
                                    linear_half(l, tiles[0])
                            if l == 0:
                                distances(u, 3)
                            if tiles:
                                gate_half(l, tiles[1])
                                linear_half(l, tiles[1])
                            else:
                                down_half(l, 0)
                                down_half(l, 1)
                            normalise(u)
                        if l == 0:
                            down_half(0, 0)
                            down_half(0, 1)
                        else:
                            rms()
                        update_x(l)

                def weigh(pool, u, i):
                    _, tiles = tiles_of_unit(u)
                    if not tiles or not gated(1, tiles[i]):
                        return
                    j = tiles[i]
                    n = j - SHARED_T
                    pool.wait_ge(s_h, tile0[1] + j + 1)
                    loads = sum(1 + len([r for r in range(EH, NE * EH, EH) if P * m < r < P * m + P])
                                for m in range(n % 2, n + 1, 2))
                    pool.wait_ge(s_gr[n % 2], 16 * loads)
                    nc.gpsimd.tensor_tensor(hbuf[:, j, :], hbuf[:, j, :], gring[:, n % 2, :], ALU.mult).then_inc(s_hw, 1)

                @block.gpsimd
                def _(pool):
                    for l in (0, 1):
                        pool.wait_ge(s_aggr, NT * (l + 1))
                        nc.gpsimd.tensor_scalar(rstd[:], mv[:, :, 1], EPS, None, ALU.add).then_inc(s_veps, 1)
                        pool.wait_ge(s_veps, l + 1)
                        nc.gpsimd.tensor_tensor(rstd[:], rstd[:], pw[:, 0:NT], ALU.pow).then_inc(s_rstd, 1)
                        for i, (_, _, m, _) in enumerate(PROJ[l]):
                            pool.wait_ge(s_phi, proj0[l] + i + 1)
                            nc.gpsimd.tensor_tensor(stage(i, 1)[0:m, :].bitcast(F32R), stage(i, 2)[0:m, :],
                                                    stage(i, 0)[0:m, :], ALU.subtract).then_inc(s_plo, 1)
                    for u in range(UNITS[0], U_ALL):
                        for kt in range(NT):
                            pool.wait_ge(s_exp, PACKS * u + (4, 8, 10, 11)[kt])
                            pr = probs[:, kt % 2, :, 0:P]
                            nc.gpsimd.affine_select(pr, pr, [[0, G4], [1, P]], ALU.is_ge, 0.0, base=0,
                                                    channel_multiplier=-1).then_inc(s_pm, 1)
                            if u > UNITS[0] and kt == 0:
                                weigh(pool, u - 1, 1)
                        weigh(pool, u, 0)
                    pool.wait_ge(s_rm, 3)
                    nc.gpsimd.tensor_scalar(srstd[:], ssum[:], 1.0 / DV, EPS, ALU.mult, ALU.add).then_inc(s_rmp, 1)
                    pool.wait_ge(s_rmp, 1)
                    nc.gpsimd.tensor_tensor(srstd[:], srstd[:], pw[:], ALU.pow).then_inc(s_rmp, 1)

            nc.all_engine_barrier()
            for s in body_sems:
                nc.sync.sem_clear(s)
            nc.all_engine_barrier()


def kernel(**inputs):
    import numpy as np
    import concourse.bacc as bacc
    from concourse.bass_utils import run_bass_kernel_spmd

    a = {k: np.asarray(v) for k, v in inputs.items()}

    def chunks(w):
        return np.ascontiguousarray(w.T.reshape(KC, P, -1).transpose(1, 0, 2))

    def up_tiles(gate, lin):
        both = np.stack([gate, lin]).reshape(2, -1, P, KC, P)
        return np.ascontiguousarray(both.transpose(1, 4, 0, 3, 2))

    def down_tiles(w):
        return np.ascontiguousarray(w.T.reshape(-1, P, C).transpose(1, 0, 2))

    hs = 352
    pad = np.zeros((SHARED_T * P - hs, C), np.float32)
    gw, up, dn = a["L1_ffn_shared_gw"], a["L1_ffn_up_w"], a["L1_ffn_down_w"]
    gate1 = np.concatenate([gw[hs:], pad, up[:, :EH].reshape(-1, C)])
    lin1 = np.concatenate([gw[:hs], pad, up[:, EH:].reshape(-1, C)])
    down1 = np.concatenate([a["L1_ffn_shared_dw"], pad.T, dn.transpose(1, 0, 2).reshape(C, -1)], axis=1)

    had = np.ones((1, 1), np.float32)
    while had.shape[0] < P:
        had = np.block([[had, had], [had, -had]])
    d = np.arange(T)[None, :] - np.arange(P)[:, None]
    dist = np.where(d >= 0, np.sqrt(np.maximum(d, 0)), 1.0e30).astype(np.float32)
    causal = np.where(np.arange(P)[None, :] <= np.arange(P)[:, None], 0.0, -BIG).astype(np.float32)
    arrays = {
        "x": a["L0_attn_x"].reshape(B * T, C),
        "w0_qk": chunks(np.concatenate([a["L0_attn_Wq"], a["L0_attn_Wk"]])),
        "w0_v": chunks(a["L0_attn_Wv"]),
        "w0_o": chunks(a["L0_attn_Wo"]),
        "w0_up": np.ascontiguousarray(up_tiles(a["L0_ffn_W1"], a["L0_ffn_W3"]).transpose(1, 0, 2, 3, 4)),
        "w0_down": down_tiles(a["L0_ffn_W2"]),
        "w1_qk": chunks(np.concatenate([a["L1_attn_Wq"], a["L1_attn_Wk"]])),
        "w1_v": chunks(a["L1_attn_Wv"]),
        "w1_o": chunks(a["L1_attn_Wo"]),
        "w1_up": up_tiles(gate1, lin1),
        "w1_down": down_tiles(down1),
        "w1_gate": chunks(a["L1_ffn_gate_w"]),
        "gate_bias": a["L1_ffn_gate_bias"],
        "lambdas": np.concatenate([a[f"L1_attn_lambda_{n}"] for n in ("q1", "k1", "q2", "k2")]),
        "subln": a["L1_attn_subln_weight"],
        "c_ident": np.eye(P, dtype=np.float32),
        "c_hadamard": (had / 32).astype(np.float32),
        "c_dist": dist,
        "c_causal": causal,
    }
    nc = bacc.Bacc("TRN2", target_bir_lowering=False, num_devices=1)
    args = [nc.dram_tensor("in_" + n, v.shape, mybir.dt.from_np(v.dtype), kind="ExternalInput").ap() for n, v in arrays.items()]
    out = nc.dram_tensor("out", (B * T, C), F32, kind="ExternalOutput").ap()
    gated_layers_kernel(nc, *args, out)
    r = run_bass_kernel_spmd(nc, [{"in_" + n: v for n, v in arrays.items()}], core_ids=[0])
    return r.results[0]["out"].reshape(B, T, C)
```

```python
import math
from contextlib import ExitStack

import concourse.bass as bass
from concourse import mybir

F32 = mybir.dt.float32
F32R = mybir.dt.float32r
BF16 = mybir.dt.bfloat16
I32 = mybir.dt.int32
ALU = mybir.AluOpType
ACT = mybir.ActivationFunctionType
AX = mybir.AxisListType

P = 128
T = 512
NT = T // P
C = 256
KC = C // P
B = 8
G4 = 4
UNITS = (4, 8)
U0 = (0, UNITS[0])
U_ALL = sum(UNITS)
DH = (16, 8)
DV = 16
NV = (4, 16)
ROWS = (48, 32)
EXP_SCALE = (1.0 / math.sqrt(16), 1.0 / math.sqrt(8))
HT = (8, 14)
J_ALL = sum(HT)
SHARED_T = 3
NE = 8
EH = 176
EPS = 1e-5
LAMBDA_INIT = 0.8 - 0.6 * math.exp(-0.3 * 12)
BIG = 3.0e38
QK_MAX = 1.0e18
RSQRT_MAGIC = 1597463007.0
MROW = P - 1
PACKS = 11
SCORE_PACKS = [(0, g, 1) for g in range(4)] + [(1, g, 1) for g in range(4)] + [(2, 0, 2), (2, 2, 2), (3, 0, 4)]
MAX_PACKS = [(3, g, 1) for g in range(4)] + [(2, g, 1) for g in range(4)] + [(1, 0, 2), (1, 2, 2), (0, 0, 4)]
PACKS_TO = (4, 8, 10, 11)
SLOPES = [float((2.0 ** -0.5) ** (h + 1)) for h in range(16)]
TILE_IN = {0: 0, 1: 2, 2: 4, 3: 6, 4: 13}
TILE_AFTER = {0: 1, 1: 3, 2: 5, 3: 7, 4: 14, 5: 15, 6: 16, 7: 17, 8: 18, 9: 19, 10: 20, 11: 21}
FRONT_TILES = (8, 9, 10, 11, 12)
UP_SLOTS = 3
RMS_STEPS = 17
PROJ = [
    [(True, 0, 128, 0), (False, 256, 64, 0), (True, 128, 128, 8)],
    [(True, 0, 128, 0), (False, 256, 128, 0), (True, 128, 128, 16), (False, 384, 128, 16)],
]
PASSES = ((0, 0), (0, 1), (1, 0))
UP_STEPS = KC * len(PASSES)


def layer_of(u):
    return 0 if u < UNITS[0] else 1


def last_of_layer(u):
    return u in (UNITS[0] - 1, U_ALL - 1)


def layer_tile(j):
    return (0, j) if j < HT[0] else (1, j - HT[0])


def gate_segments(n):
    r, out = P * n, []
    while r < P * n + P:
        e = r // EH
        m = min(EH * (e + 1), P * n + P) - r
        out.append((e, r - P * n, m))
        r += m
    return out


def gated_layers_kernel(nc, x_in, w0_qk, w0_v, w0_o, w_up, w0_down, w1_qk, w1_v, w1_o, w1_down,
                        w1_gate, gate_bias, lambdas, subln, c_ident, c_hadamard, c_dist, c_causal, out):
    with ExitStack() as ctx:
        def sb(name, shape, dt=F32):
            return ctx.enter_context(nc.sbuf_tensor(name, shape, dt))

        def sem(name):
            s = ctx.enter_context(nc.semaphore(name))
            body_sems.append(s)
            return s

        def clear_all():
            first, last = body_sems[0].num, body_sems[-1].num
            assert last - first + 1 == len(body_sems)
            nc.sync.sem_clear(range(first, last + 1))

        body_sems = []
        dram = lambda name, shape: nc.dram_tensor(name, shape, F32, kind="Internal").ap()
        q_img = [dram(f"q_img{l}", [UNITS[l] * G4, ROWS[l], T]) for l in (0, 1)]
        k_img = [dram("k_img0", [4, ROWS[0], T]), dram("k_img1", [32, ROWS[1], T])]
        gate_img = dram("gate_img", [NE, T])
        up_img = dram("up_img", [J_ALL, P, 2 * T])

        wqk = [sb("wqk0", [P, 2, KC, 320], F32R), sb("wqk1", [P, 2, KC, 512], F32R)]
        wv = [sb("wv0", [P, 2, KC, 64], F32R), sb("wv1", [P, 2, KC, 256], F32R)]
        wgate = sb("wgate", [P, 2, KC, NE], F32R)
        wo = [sb("wo0", [P, KC, C]), sb("wo1", [P, KC, C])]
        wdown = [sb("wdown0", [P, HT[0], C]), sb("wdown1", [P, HT[1], C])]
        bias_e = sb("bias_e", [P, NE])
        lam_in = sb("lam_in", [P, 4, 8])
        lam = sb("lam", [P, 8])
        gln = sb("gln", [P, DV])
        ident = sb("ident", [P, P])
        ident_bf = sb("ident_bf", [P, P], BF16)
        causal_bf = sb("causal_bf", [P, G4, P], BF16)
        dist = sb("dist", [P, T])
        minus_half = sb("minus_half", [P, 4])
        qring = [sb("qring0", [P, 2, G4, T], F32R), sb("qring1", [P, 2, G4, T], F32R)]
        kring = [sb("kring0", [P, 2, T], F32R), sb("kring1", [P, 2, T], F32R)]
        upring = sb("upring", [P, UP_SLOTS, 2, 2, KC, P], F32R)
        gring = sb("gring", [P, 2, T])
        hbuf = sb("hbuf", [P, HT[1], T])
        probs = sb("probs", [P, 2, G4, T])
        slots = probs[:].rearrange("p a g n -> p (a g) n")
        xin = sb("xin", [P, NT, C])
        x = sb("x", [P, NT, C])
        xn = [sb("xn0", [P, NT, C]), sb("xn1", [P, NT, C])]
        xnT = [sb("xnT0", [P, 2, KC, T], F32R), sb("xnT1", [P, 2, KC, T], F32R)]
        v = [sb("v0", [P, NT, NV[0], DV + 1]), sb("v1", [P, NT, NV[1], DV + 1])]
        shared8 = sb("shared8", [P, 2048])
        estrip = shared8[:].rearrange("p (g n) -> p g n", g=G4)
        on = shared8[:].rearrange("p (t h d) -> p t h d", t=NT, h=32)
        o_sb = xn
        oT = slots[:, 6:8, :]
        ot = sb("ot", [P, T])
        tb = sb("tb", [P, T])
        fo = sb("fo", [P, NT, C])
        stats = sb("stats", [P, NT, 6])
        mv = sb("mv", [P, NT, 2])
        rstd = sb("rstd", [P, NT])
        rden = sb("rden", [P, 16])
        nmax = sb("nmax", [P, 2, NT, G4])
        mneg = sb("mneg", [G4, T], F32R)
        rt = sb("rt", [P, 6, NT, NE])
        rs = sb("rs", [P, NT])
        gT = sb("gT", [NE, T])
        nw = sb("nw", [P, 4, 64])

        bank = [ctx.enter_context(nc.psum_tensor(f"bank{i}", [P, 512], F32)) for i in range(8)]
        MX, SC, PV, MISC, FB = bank[0:2], bank[2:4], bank[4], bank[5], bank[6:8]

        s_zero = sem("zeros_ready")
        s_pad = sem("image_padding_written")
        s_ones = sem("image_ones_written")
        s_kones = sem("ring_ones_written")
        s_uin = [sem(f"up_weights_in_{i}") for i in range(4)]
        s_uhi = sem("up_weights_high")
        s_ulo = sem("up_weights_low")
        s_uout = [sem(f"up_weights_out_{i}") for i in range(4)]
        s_raw = sem("raw_weights_loaded")
        s_rhi = sem("weights_high")
        s_wd = sem("down_weights_loaded")
        s_small = sem("constants_loaded")
        s_big = sem("other_weights_loaded")
        s_fw = sem("butterflies_done")
        s_had = sem("hadamard_products_ready")
        s_hade = sem("hadamard_products_copied")
        s_lam = sem("lambda_steps")
        s_lamx = sem("lambda_exps")
        s_pvz = sem("pv_bank_zeroed")
        tmp8 = hbuf[:, 8:12, :].rearrange("p a n -> p (a n)").rearrange("p (t n) -> p t n", t=HT[0])
        zero_t = hbuf[:, 12:14, :]
        ones_row = ot[:]
        hadamard = tb[:, 0:P]
        causal_f = tb[:, P:2 * P]
        n_ustage = 4
        raw = [(slots[:, 0:2, :].rearrange("p a n -> p (a n)")[:, 0:640], wqk[0], w0_qk),
               (slots[:, 2:4, :].rearrange("p a n -> p (a n)")[:, 0:1024], wqk[1], w1_qk),
               (slots[:, 4, 0:128], wv[0], w0_v), (slots[:, 5, 0:512], wv[1], w1_v), (slots[:, 6, 0:16], wgate, w1_gate)]
        with nc.Block() as block:
            @block.sync
            def _(sp):
                sp.dma_start(wdown[0][:], w0_down).then_inc(s_wd, 16)
                for t in range(n_ustage):
                    sp.dma_start(hbuf[:, 2 * t + 1, :], w_up[t]).then_inc(s_uin[t], 16)
                for dst, _, src in raw:
                    sp.dma_start(dst, src.rearrange("p k n -> p (k n)")).then_inc(s_raw, 16)
                for dst, src in ((ident[:], c_ident), (hadamard, c_hadamard), (causal_f, c_causal),
                                 (bias_e[:], gate_bias.partition_broadcast(P)),
                                 (lam_in[:].rearrange("p a b -> p (a b)"), lambdas.partition_broadcast(P)),
                                 (gln[:], subln.partition_broadcast(P))):
                    sp.dma_start(dst, src).then_inc(s_small, 16)
                for t in range(J_ALL):
                    s = t % n_ustage
                    sp.wait_ge(s_uhi, t + 1)
                    sp.wait_ge(s_ulo, t + 1)
                    sp.dma_start(up_img[t], hbuf[:, 2 * s:2 * s + 2, :].rearrange("p a n -> p (a n)"))\
                        .then_inc(s_uout[s], 16)
                    if t >= 1 and t + n_ustage - 1 < J_ALL:
                        n = t + n_ustage - 1
                        sp.wait_ge(s_uout[n % n_ustage], 16 * (n // n_ustage))
                        sp.dma_start(hbuf[:, 2 * (n % n_ustage) + 1, :], w_up[n]).then_inc(s_uin[n % n_ustage], 16)
                for s in range(n_ustage):
                    sp.wait_ge(s_uout[s], 16 * len(range(s, J_ALL, n_ustage)))

            @block.gpsimd
            def _(pool):
                for dst, src in ((dist[:], c_dist), (wo[0][:], w0_o), (wo[1][:], w1_o), (wdown[1][:], w1_down)):
                    nc.gpsimd.dma_start(dst, src).then_inc(s_big, 16)
                pool.wait_ge(s_zero, 1)
                for img in (q_img[1], k_img[1]):
                    nc.gpsimd.dma_start(img[:, 24:32, :], zero_t).then_inc(s_pad, 16)
                pool.wait_ge(s_pad, 32)
                nc.gpsimd.dma_start(k_img[1][3:32:4, 31, :], ones_row[0:8, :]).then_inc(s_ones, 16)
                pool.wait_ge(s_ones, 16)
                pool.wait_ge(s_big, 64)

            @block.vector
            def _(dve):
                nc.vector.memset(zero_t, 0.0)
                nc.vector.memset(ones_row, 1.0).then_inc(s_zero, 1)
                nc.vector.memset(minus_half[:], -0.5)
                dve.wait_ge(s_wd, 16)
                src, dst = wdown[0][:], tmp8
                n = 0
                for b in (1, 2, 4):
                    for i in range(0, HT[0], 2 * b):
                        lo, hi = slice(i, i + b), slice(i + b, i + 2 * b)
                        nc.vector.tensor_tensor(dst[:, lo, :], src[:, lo, :], src[:, hi, :], ALU.add).then_inc(s_fw, 1)
                        nc.vector.tensor_tensor(dst[:, hi, :], src[:, lo, :], src[:, hi, :],
                                                ALU.subtract).then_inc(s_fw, 1)
                        n += 2
                    dve.wait_ge(s_fw, n)
                    src, dst = dst, src
                dve.wait_ge(s_raw, 16 * len(raw))
                for i, (stage, w, _) in enumerate(raw):
                    dve.wait_ge(s_rhi, i + 1)
                    nc.vector.tensor_tensor(w[:, 1].rearrange("p k n -> p (k n)"), stage,
                                            w[:, 0].rearrange("p k n -> p (k n)").bitcast(F32), ALU.subtract)
                for t in range(J_ALL):
                    s = t % n_ustage
                    dve.wait_ge(s_uhi, t + 1)
                    nc.vector.tensor_tensor(hbuf[:, 2 * s + 1, :].bitcast(F32R), hbuf[:, 2 * s + 1, :], hbuf[:, 2 * s, :],
                                            ALU.subtract).then_inc(s_ulo, 1)
                for l in (0, 1):
                    nc.vector.memset(qring[l][:].rearrange("p a g n -> p (a g n)").bitcast(F32), 0.0)
                    nc.vector.memset(v[l][:].rearrange("p t h d -> p (t h d)"), 1.0)
                nc.vector.memset(kring[0][:].rearrange("p a n -> p (a n)").bitcast(F32), 0.0).then_inc(s_zero, 1)
                nc.vector.memset(rt[:].rearrange("p a t e -> p (a t e)"), BIG)
                dve.wait_ge(s_small, 96)
                nc.vector.tensor_copy(ident_bf[:], ident[:])
                nc.vector.tensor_copy(causal_bf[:], causal_f.unsqueeze(1).to_broadcast([P, G4, P]))
                for i in (0, 1):
                    nc.vector.tensor_tensor(lam_in[:, 2 * i, :], lam_in[:, 2 * i, :], lam_in[:, 2 * i + 1, :],
                                            ALU.mult).then_inc(s_lam, 1)
                dve.wait_ge(s_lam, 2)
                nc.vector.tensor_reduce(lam[:, 0:2], lam_in[:, 0:4:2, :], AX.X, ALU.add).then_inc(s_lam, 1)
                dve.wait_ge(s_lamx, 1)
                nc.vector.tensor_tensor(lam[:, 4:5], lam[:, 3:4], lam[:, 2:3], ALU.subtract).then_inc(s_lam, 1)
                dve.wait_ge(s_lam, 4)
                nc.vector.tensor_scalar(lam[:, 5:6], lam[:, 4:5], -LAMBDA_INIT, None, ALU.add)
                nc.vector.tensor_scalar(gln[:], gln[:], 1.0 - LAMBDA_INIT, None, ALU.mult)

            @block.scalar
            def _(act):
                act.wait_ge(s_raw, 16 * len(raw))
                for stage, w, _ in raw:
                    nc.scalar.copy(w[:, 0].rearrange("p k n -> p (k n)"), stage).then_inc(s_rhi, 1)
                for t in range(J_ALL):
                    s = t % n_ustage
                    act.wait_ge(s_uin[s], 16 * (t // n_ustage + 1))
                    nc.scalar.copy(hbuf[:, 2 * s, :].bitcast(F32R), hbuf[:, 2 * s + 1, :]).then_inc(s_uhi, 1)
                for t in range(HT[0]):
                    act.wait_ge(s_had, t + 1)
                    nc.scalar.copy(wdown[0][:, t, :], bank[t % 4][:, 0:C]).then_inc(s_hade, 1)
                act.wait_ge(s_lam, 3)
                nc.scalar.activation(lam[:, 2:4], lam[:, 0:2], ACT.Exp).then_inc(s_lamx, 1)

            @block.tensor
            def _(pe):
                pe.wait_ge(s_fw, 14)
                pe.wait_ge(s_small, 96)
                for t in range(HT[0]):
                    if t >= 4:
                        pe.wait_ge(s_hade, t - 3)
                    nc.tensor.matmul(bank[t % 4][:, 0:C], hadamard, tmp8[:, t, :], start=True, stop=True).then_inc(s_had, 1)
                pe.wait_ge(s_zero, 1)
                nc.tensor.matmul(PV[:], zero_t[:, 0, 0:P], zero_t[:, 0, :], start=True, stop=True)

        with nc.Block() as block:
            @block.sync
            def _(sp):
                for s in (0, 1):
                    sp.dma_start(kring[0][MROW:MROW + 1, s, :].bitcast(F32), ones_row[0:1, :]).then_inc(s_kones, 16)
                sp.wait_ge(s_kones, 32)
        nc.gpsimd.dma_reset()
        nc.all_engine_barrier()
        clear_all()
        body_sems.clear()

        two = lambda name: [sem(f"{name}_{l}") for l in (0, 1)]
        s_x = sem("x_loaded")
        s_stat, s_aggr, s_veps, s_rstd = two("stats_ready"), two("moments_ready"), two("var_plus_eps"), two("rstd_ready")
        s_xn, s_xnTp, s_xnhi, s_xnlo = two("xn_ready"), two("xnT_in_psum"), two("xnT_high_ready"), two("xnT_low_ready")
        s_proj, s_pc = two("projection_in_psum"), two("projection_copied")
        s_phi, s_plo = two("projection_high_ready"), two("projection_low_ready")
        s_img = [[sem(f"image_written_{l}_{i}") for i in range(len(PROJ[l]))] for l in (0, 1)]
        s_vp, s_v = two("v_in_psum"), two("v_ready")
        s_rp = sem("router_logits_in_psum")
        s_rtk = sem("router_steps")
        s_rsg = sem("router_tanh_ready")
        s_rT = sem("router_weights_transposed")
        s_rTc = sem("router_weights_copied")
        s_rimg = sem("router_weights_written")
        s_mp, s_mr, s_mT = two("max_scores_in_psum"), two("max_reduced"), two("max_transposed")
        s_mc, s_mrow = two("max_copied"), two("max_row_loaded")
        s_ring = {u: sem(f"ring_of_unit_{u}_loaded") for u in (0, 1)}
        s_ringn = [sem("ring_even_loaded"), sem("ring_odd_loaded")]
        s_sc = sem("scores_in_psum")
        s_exp = sem("exps_ready")
        s_es = sem("distance_factors_ready")
        s_pm = sem("probs_masked")
        s_pc3 = sem("last_heads_probs_causal")
        s_pm3 = sem("last_heads_probs_masked")
        s_pv = sem("pv_done")
        s_ot = sem("pv_copied")
        s_oTp = sem("outputs_transposed")
        s_rd = sem("denominators_inverted")
        s_on = sem("outputs_normalised")
        s_up = [sem(f"up_weights_loaded_{i}") for i in range(UP_SLOTS)]
        s_uppre = sem("next_up_weights_loaded")
        s_gr = [sem("expert_weights_loaded_even"), sem("expert_weights_loaded_odd")]
        s_g = sem("gate_half_in_psum")
        s_u = sem("linear_half_in_psum")
        s_t = sem("tanh_ready")
        s_gu = sem("gate_half_used")
        s_h = sem("hidden_ready")
        s_hw = sem("hidden_weighted")
        s_dn = sem("down_in_psum")
        s_fo = sem("ffn_silu_ready")
        s_rm = sem("rms_steps")
        s_oTt = sem("o_transposed_in_psum")
        s_oTs = sem("oT_ready")
        s_so = sem("attention_out_in_psum")
        s_gx = sem("gated_ready")
        s_xr = sem("x_updated")
        s_out = sem("out_written")

        def stage(i, part):
            return slots[:, 2 * i + part, :]

        def wait_images(eng, l, tiles):
            for i in range(tiles):
                eng.wait_ge(s_img[l][i], 48)

        def mx(u):
            return (0, 0) if u == 0 else (1, u - 1)

        def load_x(sp, t0):
            sp.dma_start(xin[:], x_in[t0, :].rearrange("(t p) c -> p t c", p=P)).then_inc(s_x, 16)

        def write_images(sp, l, tiles):
            for i in tiles:
                is_q, _, m, h0 = PROJ[l][i]
                d = DH[l]
                img = (q_img if is_q else k_img)[l][h0:h0 + m // d]
                sp.wait_ge(s_phi[l], i + 1)
                sp.wait_ge(s_plo[l], i + 1)
                for t, part in enumerate((0, 0, 1) if is_q else (0, 1, 0)):
                    sp.dma_start(img[:, d * t:d * t + d, :], stage(i, part)[0:m, :]).then_inc(s_img[l][i], 16)

        def ring_load(sp, u):
            l = layer_of(u)
            w = u - U0[l]
            s = u % 2
            done = s_ring[u] if u < 2 else s_ringn[s]
            if l == 0:
                if w < 2:
                    wait_images(sp, 0, 2)
                sp.dma_start(qring[0][0:48, s, :, :].bitcast(F32),
                             q_img[0][4 * w:4 * w + 4].rearrange("g r n -> r g n")).then_inc(done, 16)
                sp.dma_start(kring[0][0:48, s, :].bitcast(F32), k_img[0][w]).then_inc(done, 16)
            else:
                wait_images(sp, 1, 2 if w < 4 else 4)
                for g in range(G4):
                    sp.dma_start(qring[1][32 * g:32 * g + 32, s, g, :].bitcast(F32), q_img[1][4 * w + g]).then_inc(done, 16)
                sp.dma_start(kring[1][:, s, :].bitcast(F32),
                             k_img[1][4 * w:4 * w + 4].rearrange("g r n -> (g r) n")).then_inc(done, 16)

        def wait_ring(eng, u):
            if u == 0:
                eng.wait_ge(s_ring[0], 32)
            elif u >= 2:
                eng.wait_ge(s_ringn[u % 2], 16 * sum(2 if layer_of(i) == 0 else 5 for i in range(2 + u % 2, u + 1, 2)))

        def max_row(sp, u):
            k, n = mx(u)
            sp.wait_ge(s_mc[k], n + 1)
            sp.dma_start(qring[layer_of(u)][MROW:MROW + 1, u % 2, :, :].bitcast(F32),
                         mneg[:].bitcast(F32)).then_inc(s_mrow[k], 16)

        def up_load(sp, j, done=None):
            if j >= UP_SLOTS:
                sp.wait_ge(s_u, j - UP_SLOTS + 1)
            sp.dma_start(upring[:, j % UP_SLOTS].rearrange("p a h k n -> p (a h k n)").bitcast(F32), up_img[j])\
                .then_inc(done or s_up[j % UP_SLOTS], 16)

        def product(out_ap, a, b, part_a, part_b, first=0, count=KC * len(PASSES)):
            steps = [(k, pa, pb) for k in range(KC) for pa, pb in PASSES]
            for n in range(first, first + count):
                k, pa, pb = steps[n]
                last = nc.tensor.matmul(out_ap, part_a(a, pa, k), part_b(b, pb, k), start=(n == 0),
                                        stop=(n == len(steps) - 1))
            return last

        def pe_turn(pe, l, half):
            pe.wait_ge(s_xn[l], half + 1)
            if half:
                pe.wait_ge(s_xnlo[l], KC)
            for k in range(KC):
                for tt in (2 * half, 2 * half + 1):
                    last = nc.tensor.transpose(MX[k][:, tt * P:(tt + 1) * P], xn[l][:, tt, k * P:(k + 1) * P], ident[:])
            last.then_inc(s_xnTp[l], 1)

        def pe_project(pe, l, i):
            _, c0, m, _ = PROJ[l][i]
            if l == 0 and i == 2:
                pe.wait_ge(s_pc[0], 1)
            bk = [[MX[0], MX[1], MX[0]], [SC[0], SC[1], MX[0], MX[1]]][l][i]
            product(bk[0:m, :], wqk[l], xnT[l], lambda w, p, k: w[:, p, k, c0:c0 + m],
                    lambda t, p, k: t[:, p, k, :]).then_inc(s_proj[l], 1)

        def pe_v(pe, l):
            w = DV * NV[l]
            if l == 0:
                pe.wait_ge(s_pc[0], 2)
            for tt in range(NT):
                o = MX[1][:, tt * w:(tt + 1) * w] if l == 0 else (PV, MISC)[tt // 2][:, (tt % 2) * w:(tt % 2 + 1) * w]
                last = product(o, xnT[l], wv[l], lambda t, p, k: t[:, p, k, tt * P:(tt + 1) * P],
                               lambda w_, p, k: w_[:, p, k, :])
            last.then_inc(s_vp[l], 1)

        def pe_max_pack(pe, u, i):
            l, s = layer_of(u), u % 2
            k, before = mx(u)
            n = PACKS * before + i
            qt, g0, heads = MAX_PACKS[i]
            w = P * (qt + 1)
            if n >= 2:
                pe.wait_ge(s_mr[k], n - 1)
            bk = MX[n % 2]
            for g in range(g0, g0 + heads):
                nc.tensor.matmul(bk[:, (g - g0) * w:(g - g0 + 1) * w], qring[l][0:MROW, s, g, qt * P:(qt + 1) * P],
                                 kring[l][0:MROW, s, 0:w], start=True, stop=True)
            diag = bk[:, 0:heads * w].rearrange("p (g n) -> p g n", g=heads)[:, :, qt * P:w]
            nc.tensor.matmul(diag, ident_bf[:], causal_bf[:, 0:heads, :], start=False, stop=True,
                             skip_group_check=True).then_inc(s_mp[k], 1)

        def pe_max_turn(pe, u):
            k, n = mx(u)
            pe.wait_ge(s_mr[k], PACKS * (n + 1))
            for qt in range(NT):
                last = nc.tensor.transpose(MISC[0:G4, qt * P:(qt + 1) * P], nmax[:, u % 2, qt, :], ident[:])
            last.then_inc(s_mT[k], 1)

        def pe_score_pack(pe, u, i):
            l, s = layer_of(u), u % 2
            n = PACKS * u + i
            kt, g0, heads = SCORE_PACKS[i]
            w = T - P * kt
            if n >= 2:
                pe.wait_ge(s_exp, n - 1)
            if i == 0 and u:
                pe.wait_ge(s_mrow[1], 16 * u)
            for g in range(g0, g0 + heads):
                last = nc.tensor.matmul(SC[n % 2][:, (g - g0) * w:(g - g0 + 1) * w],
                                        kring[l][:, s, kt * P:(kt + 1) * P],
                                        qring[l][:, s, g, kt * P:T], start=True, stop=True)
            last.then_inc(s_sc, 1)

        def pe_pv(pe, u, kt):
            l = layer_of(u)
            pe.wait_ge(s_pm, 4 * u + kt + 1)
            if l == 0:
                pe.wait_ge(s_pm3, 4 * u + kt + 1)
            if kt == 0 and u:
                pe.wait_ge(s_ot, u)
            for g in range(G4):
                hv = u if l == 0 else 2 * (u - U0[1]) + g // 2
                last = nc.tensor.matmul(PV[32 * g:32 * g + DV + 1, kt * P:T], v[l][:, kt, hv, :],
                                        probs[:, kt % 2, g, 0:T - P * kt], start=(kt == 0),
                                        stop=(kt == NT - 1), skip_group_check=True)
            last.then_inc(s_pv, 1)

        def pe_out_turn(pe, u):
            pe.wait_ge(s_ot, u + 1)
            if not last_of_layer(u):
                pe.wait_ge(s_mc[1], u + 1)
            else:
                pe.wait_ge(s_on, u)
            for tt in range(NT):
                last = nc.tensor.transpose(MISC[:, tt * P:(tt + 1) * P], ot[:, tt * P:(tt + 1) * P], ident[:])
            last.then_inc(s_oTp, 1)

        def pe_up(pe, j, half, first=0, count=UP_STEPS):
            l, _ = layer_tile(j)
            if first == 0:
                if j:
                    pe.wait_ge((s_gu, s_h)[half], j)
                if j == HT[0]:
                    pe.wait_ge(s_fo, half + 1)
                if half == 0 and j >= UP_SLOTS:
                    pe.wait_ge(s_up[j % UP_SLOTS], 16 * (j // UP_SLOTS))
            last = product(FB[half][:], upring, xnT[l], lambda w, p, k: w[:, j % UP_SLOTS, p, half, k, :],
                           lambda t, p, k: t[:, p, k, :], first, count)
            if first + count == UP_STEPS:
                last.then_inc((s_g, s_u)[half], 1)

        def pe_up_between(pe, j, i):
            for n in range(2 * UP_STEPS * i // PACKS, 2 * UP_STEPS * (i + 1) // PACKS):
                pe_up(pe, j, n // UP_STEPS, n % UP_STEPS, 1)

        def pe_down(pe, l, tt, part=None):
            js = range(HT[l]) if part is None else part
            if tt == 0:
                pe.wait_ge(s_h, (HT[0], J_ALL)[l])
                if l == 1:
                    pe.wait_ge(s_hw, HT[1] - SHARED_T)
            for j in js:
                last = nc.tensor.matmul(FB[tt // 2][:, (tt % 2) * C:(tt % 2 + 1) * C], hbuf[:, j, tt * P:(tt + 1) * P],
                                        wdown[l][:, j, :], start=(j == 0), stop=(j == HT[l] - 1))
            if tt % 2 and js[-1] == HT[l] - 1:
                last.then_inc(s_dn, 1)

        def pe_o_turn(pe, l):
            pe.wait_ge(s_on, (UNITS[0], U_ALL)[l])
            if l == 1:
                pe.wait_ge(s_rm, RMS_STEPS)
            for k in range(KC):
                for tt in range(NT):
                    last = nc.tensor.transpose((PV, MISC)[k][:, tt * P:(tt + 1) * P], o_sb[l][:, tt, k * P:(k + 1) * P],
                                               ident[:])
                last.then_inc(s_oTt, 1)

        def pe_attention_out(pe, l, half):
            pe.wait_ge(s_oTs, 2 * (l + 1))
            for tt in (2 * half, 2 * half + 1):
                for k in range(KC):
                    last = nc.tensor.matmul(SC[half][:, (tt % 2) * C:(tt % 2 + 1) * C], oT[:, k, tt * P:(tt + 1) * P],
                                            wo[l][:, k, :], start=(k == 0), stop=(k == KC - 1))
            last.then_inc(s_so, 1)

        def act_turn(act, l, half):
            for k in range(KC):
                act.wait_ge(s_xnTp[l], half + 1)
                nc.scalar.copy(xnT[l][:, 0, k, half * 256:half * 256 + 256],
                               MX[k][:, half * 256:half * 256 + 256]).then_inc(s_xnhi[l], 1)

        def act_project(act, l, i):
            m = PROJ[l][i][2]
            act.wait_ge(s_pc[l], i + 1)
            nc.scalar.copy(stage(i, 0)[0:m, :].bitcast(F32R), stage(i, 1)[0:m, :]).then_inc(s_phi[l], 1)

        def act_v(act, l):
            act.wait_ge(s_vp[l], 1)
            if l == 0:
                last = nc.scalar.copy(v[0][:, :, :, 0:DV], MX[1][:, 0:256].rearrange("p (t h d) -> p t h d", t=NT, h=4))
            else:
                for i in range(2):
                    last = nc.scalar.copy(v[1][:, 2 * i:2 * i + 2, :, 0:DV],
                                          (PV, MISC)[i][:].rearrange("p (t h d) -> p t h d", t=2, h=16))
            last.then_inc(s_v[l], 1)

        def act_strips(act, u):
            for g in range(G4):
                last = nc.scalar.activation(estrip[:, g, :], dist[:], ACT.Exp, scale=-SLOPES[4 * u + g])
                if u:
                    last.then_inc(s_es, 1)

        def act_max_copy(act, u):
            k, n = mx(u)
            act.wait_ge(s_mT[k], n + 1)
            if n:
                act.wait_ge(s_mrow[1], 16 * n)
            nc.scalar.copy(mneg[:], MISC[0:G4, :]).then_inc(s_mc[k], 1)

        def act_exps(act, u, i):
            n = PACKS * u + i
            kt, g0, heads = SCORE_PACKS[i]
            w = T - P * kt
            act.wait_ge(s_sc, n + 1)
            if 4 * u + kt >= 2:
                act.wait_ge(s_pv, 4 * u + kt - 1)
            if u == U0[1] and i == 0:
                wait_images(act, 1, 4)
            nc.scalar.activation(probs[:, kt % 2, g0:g0 + heads, 0:w],
                                 SC[n % 2][:, 0:heads * w].rearrange("p (g n) -> p g n", g=heads),
                                 ACT.Exp, scale=EXP_SCALE[layer_of(u)]).then_inc(s_exp, 1)

        def act_tanh(act, j):
            act.wait_ge(s_g, j + 1)
            if j:
                act.wait_ge(s_gu, j)
            if j == HT[0]:
                act.wait_ge(s_fo, 2)
            nc.scalar.activation(tb[:], FB[0][:], ACT.Tanh, scale=0.5).then_inc(s_t, 1)

        def act_tanh_down(act, l, half):
            act.wait_ge(s_dn, 2 * l + half + 1)
            act.wait_ge(s_gu, (HT[0], J_ALL)[l])
            if half:
                act.wait_ge(s_fo, 2 * l + half)
            nc.scalar.activation(tb[:], FB[half][:], ACT.Tanh, scale=0.5).then_inc(s_t, 1)

        def act_pv_copy(act, u):
            act.wait_ge(s_pv, 4 * (u + 1))
            if u:
                act.wait_ge(s_oTp, u)
            nc.scalar.copy(ot[:], PV[:]).then_inc(s_ot, 1)

        def act_o_turn(act, l):
            for k in range(KC):
                act.wait_ge(s_oTt, 2 * l + k + 1)
                nc.scalar.copy(oT[:, k, :], (PV, MISC)[k][:]).then_inc(s_oTs, 1)

        def dve_norm(dve, l, half):
            src = (xin, x)[l]
            for tt in (2 * half, 2 * half + 1):
                nc.vector.bn_stats(stats[:, tt, :], src[:, tt, :]).then_inc(s_stat[l], 1)
            dve.wait_ge(s_stat[l], 2 * half + 2)
            for tt in (2 * half, 2 * half + 1):
                nc.vector.bn_aggr(mv[:, tt, :], stats[:, tt, :]).then_inc(s_aggr[l], 1)
            dve.wait_ge(s_rstd[l], half + 1)
            for tt in (2 * half, 2 * half + 1):
                last = nc.vector.tensor_scalar(xn[l][:, tt, :], src[:, tt, :], mv[:, tt, 0:1], rstd[:, tt:tt + 1],
                                               ALU.subtract, ALU.mult)
            last.then_inc(s_xn[l], 1)

        def pool_norm(pool, l, half):
            tts = slice(2 * half, 2 * half + 2)
            pool.wait_ge(s_aggr[l], 2 * half + 2)
            nc.gpsimd.tensor_scalar(rstd[:, tts], mv[:, tts, 1], EPS, None, ALU.add).then_inc(s_veps[l], 1)
            pool.wait_ge(s_veps[l], half + 1)
            nc.gpsimd.tensor_tensor(rstd[:, tts], rstd[:, tts], minus_half[:, 0:2], ALU.pow).then_inc(s_rstd[l], 1)

        def dve_turn(dve, l, half):
            for k in range(KC):
                dve.wait_ge(s_xnhi[l], 2 * half + k + 1)
                cols = slice(half * 256, half * 256 + 256)
                nc.vector.tensor_tensor(xnT[l][:, 1, k, cols], MX[k][:, cols], xnT[l][:, 0, k, cols].bitcast(F32),
                                        ALU.subtract).then_inc(s_xnlo[l], 1)

        def dve_project(dve, l, i):
            m = PROJ[l][i][2]
            bk = [[MX[0], MX[1], MX[0]], [SC[0], SC[1], MX[0], MX[1]]][l][i]
            dve.wait_ge(s_proj[l], i + 1)
            if l == 1:
                nc.vector.tensor_scalar(stage(i, 1)[0:m, :], bk[0:m, :], QK_MAX, -QK_MAX, ALU.min,
                                        ALU.max).then_inc(s_pc[1], 1)
            else:
                nc.vector.tensor_copy(stage(i, 1)[0:m, :], bk[0:m, :]).then_inc(s_pc[0], 1)

        def pool_project(pool, l, i):
            m = PROJ[l][i][2]
            pool.wait_ge(s_phi[l], i + 1)
            nc.gpsimd.tensor_tensor(stage(i, 1)[0:m, :].bitcast(F32R), stage(i, 1)[0:m, :], stage(i, 0)[0:m, :],
                                    ALU.subtract).then_inc(s_plo[l], 1)

        def dve_maxima(dve, u, i):
            qt, g0, heads = MAX_PACKS[i]
            w = P * (qt + 1)
            k, before = mx(u)
            n = PACKS * before + i
            dve.wait_ge(s_mp[k], n + 1)
            if i == 0 and before >= 2:
                dve.wait_ge(s_mT[1], before - 1)
            nc.vector.tensor_reduce(nmax[:, u % 2, qt, g0:g0 + heads],
                                    MX[n % 2][:, 0:heads * w].rearrange("p (g n) -> p g n", g=heads),
                                    AX.X, ALU.max, negate=True).then_inc(s_mr[k], 1)

        def dve_distances(dve, u, kt):
            w = T - P * kt
            dve.wait_ge(s_exp, PACKS * u + PACKS_TO[kt])
            if u:
                dve.wait_ge(s_es, u)
            pr = probs[:, kt % 2, 0:3, 0:w]
            nc.vector.scalar_tensor_tensor(pr, pr, BIG, estrip[:, 0:3, 0:w], ALU.min, ALU.mult).then_inc(s_pm, 1)

        def pool_distances(pool, u, kt):
            w = T - P * kt
            pool.wait_ge(s_exp, PACKS * u + PACKS_TO[kt])
            if u:
                pool.wait_ge(s_es, u)
            pr = probs[:, kt % 2, 3, 0:w]
            nc.gpsimd.affine_select(pr[:, 0:P], pr[:, 0:P], [[1, P]], ALU.is_ge, 0.0, base=0,
                                    channel_multiplier=-1).then_inc(s_pc3, 1)
            pool.wait_ge(s_pc3, 4 * u + kt + 1)
            nc.gpsimd.tensor_tensor(pr, pr, estrip[:, 3, 0:w], ALU.mult).then_inc(s_pm3, 1)

        def dve_gate_half(dve, j):
            dve.wait_ge(s_t, j + 1 + (2 if j >= HT[0] else 0))
            nc.vector.scalar_tensor_tensor(hbuf[:, layer_tile(j)[1], :], tb[:], 1.0, FB[0][:], ALU.add,
                                           ALU.mult).then_inc(s_gu, 1)

        def dve_linear_half(dve, j):
            dve.wait_ge(s_u, j + 1)
            dve.wait_ge(s_gu, j + 1)
            h = hbuf[:, layer_tile(j)[1], :]
            nc.vector.scalar_tensor_tensor(h, h, 0.5, FB[1][:], ALU.mult, ALU.mult).then_inc(s_h, 1)

        def dve_down_half(dve, l, half):
            dve.wait_ge(s_t, (HT[0], J_ALL + 2)[l] + half + 1)
            nc.vector.scalar_tensor_tensor(fo[:, 2 * half:2 * half + 2, :].rearrange("p t c -> p (t c)"), tb[:], 1.0,
                                           FB[half][:], ALU.add, ALU.mult).then_inc(s_fo, 1)

        def dve_normalise(dve, u):
            l = layer_of(u)
            dve.wait_ge(s_oTp, u + 1)
            m = MISC[:].rearrange("p (a c) -> p a c", c=32)
            if u:
                dve.wait_ge(s_on, u)
            nc.vector.reciprocal(rden[:], m[:, :, DV]).then_inc(s_rd, 1)
            dve.wait_ge(s_rd, u + 1)
            if l == 0:
                o = o_sb[0][:, :, 64 * u:64 * u + 64].rearrange("p t (g d) -> p t g d", g=G4)
            else:
                w = u - U0[1]
                o = on[:, :, 4 * w:4 * w + 4, :]
            nc.vector.tensor_tensor(
                o, MISC[:].rearrange("p (t g c) -> p t g c", t=NT, g=G4)[:, :, :, 0:DV],
                rden[:].rearrange("p (t g) -> p t g", t=NT).unsqueeze(3).to_broadcast([P, NT, G4, DV]),
                ALU.mult).then_inc(s_on, 1)

        def dve_router(dve):
            sc, scb, top, two_, w, rep = (rt[:, i] for i in range(6))
            dve.wait_ge(s_rsg, 1)
            nc.vector.tensor_scalar(sc, sc, 1.0, 0.5, ALU.add, ALU.mult).then_inc(s_rtk, 1)
            dve.wait_ge(s_rtk, 1)
            nc.vector.tensor_tensor(scb, sc, bias_e[:].unsqueeze(1).to_broadcast([P, NT, NE]), ALU.add).then_inc(s_rtk, 1)
            dve.wait_ge(s_rtk, 2)
            for tt in range(NT):
                last = nc.vector.max(top[:, tt, :], scb[:, tt, :])
            last.then_inc(s_rtk, 1)
            dve.wait_ge(s_rtk, 3)
            nc.vector.tensor_copy(two_[:, :, 0:2], top[:, :, 0:2]).then_inc(s_rtk, 1)
            dve.wait_ge(s_rtk, 4)
            for tt in range(NT):
                last = nc.vector.match_replace(rep[:, tt, :], two_[:, tt, :], scb[:, tt, :], -BIG)
            last.then_inc(s_rtk, 1)
            dve.wait_ge(s_rtk, 5)
            nc.vector.scalar_tensor_tensor(w, rep, -BIG, sc, ALU.is_equal, ALU.mult).then_inc(s_rtk, 1)
            dve.wait_ge(s_rtk, 6)
            nc.vector.tensor_reduce(rs[:], w, AX.X, ALU.add).then_inc(s_rtk, 1)
            dve.wait_ge(s_rtk, 7)
            nc.vector.reciprocal(rs[:], rs[:]).then_inc(s_rtk, 1)
            dve.wait_ge(s_rtk, 8)
            nc.vector.tensor_tensor(w, w, rs[:].unsqueeze(2).to_broadcast([P, NT, NE]), ALU.mult).then_inc(s_rtk, 1)

        def dve_rms(dve):
            pair = on.rearrange("p t (h two) d -> p (t h) two d", two=2)
            o3 = o_sb[1][:].rearrange("p t (h d) -> p (t h) d", d=DV)
            sq = xn[0][:].rearrange("p t (h d) -> p (t h) d", d=DV)
            ms, y, a, sh = (nw[:, i, :] for i in range(4))
            n = 0

            def step(instruction):
                nonlocal n
                n += 1
                instruction.then_inc(s_rm, 1)
                dve.wait_ge(s_rm, n)

            dve.wait_ge(s_on, U_ALL)
            step(nc.vector.scalar_tensor_tensor(o3, pair[:, :, 1, :], lam[:, 5:6], pair[:, :, 0, :], ALU.mult, ALU.add))
            dve.wait_ge(s_xnTp[0], 2)
            step(nc.vector.tensor_tensor(sq, o3, o3, ALU.mult))
            step(nc.vector.tensor_reduce(ms, sq, AX.X, ALU.add))
            step(nc.vector.tensor_scalar(ms, ms, 1.0 / DV, EPS, ALU.mult, ALU.add))
            step(nc.vector.tensor_scalar(sh.bitcast(I32), ms.bitcast(I32), 1, None, ALU.arith_shift_right))
            step(nc.vector.tensor_scalar(y.bitcast(I32), sh.bitcast(I32), -1.0, RSQRT_MAGIC, ALU.mult, ALU.add))
            for _ in range(3):
                step(nc.vector.tensor_tensor(a, y, y, ALU.mult))
                step(nc.vector.scalar_tensor_tensor(a, a, -0.5, ms, ALU.mult, ALU.mult))
                step(nc.vector.scalar_tensor_tensor(y, a, 1.5, y, ALU.add, ALU.mult))
            step(nc.vector.tensor_tensor(o3, o3, y.unsqueeze(2).to_broadcast([P, 64, DV]), ALU.mult))
            nc.vector.tensor_tensor(o3, o3, gln[:].unsqueeze(1).to_broadcast([P, 64, DV]), ALU.mult).then_inc(s_rm, 1)
            assert n + 1 == RMS_STEPS

        def dve_update_x(dve, l, half):
            dve.wait_ge(s_so, 2 * l + half + 1)
            dve.wait_ge(s_fo, 2 * l + half + 1)
            tts = slice(2 * half, 2 * half + 2)
            f = fo[:, tts, :].rearrange("p t c -> p (t c)")
            nc.vector.scalar_tensor_tensor(f, SC[half][:], 0.5, f, ALU.mult, ALU.mult).then_inc(s_gx, 1)
            dve.wait_ge(s_gx, 2 * l + half + 1)
            nc.vector.tensor_tensor(x[:, tts, :], (xin, x)[l][:, tts, :], fo[:, tts, :], ALU.add).then_inc(s_xr, 1)
            dve.wait_ge(s_xr, 2 * l + half + 1)

        with nc.Block() as block:
            @block.sync
            def _(sp):
                load_x(sp, slice(0, T))
                for j in range(UP_SLOTS):
                    up_load(sp, j, s_uppre)
                write_images(sp, 0, range(3))
                ring_load(sp, 0)
                ring_load(sp, 1)
                max_row(sp, 0)
                wait_images(sp, 0, 3)
                sp.wait_ge(s_ring[1], 32)
                sp.wait_ge(s_uppre, 16 * UP_SLOTS)
                sp.wait_ge(s_mrow[0], 16)

            @block.tensor
            def _(pe):
                for half in (0, 1):
                    pe_turn(pe, 0, half)
                pe.wait_ge(s_xnlo[0], 2 * KC)
                for i in range(3):
                    pe_project(pe, 0, i)
                pe_v(pe, 0)
                wait_ring(pe, 0)
                pe.wait_ge(s_v[0], 1)
                for i in range(PACKS):
                    pe_max_pack(pe, 0, i)
                pe_max_turn(pe, 0)

            @block.scalar
            def _(act):
                for half in (0, 1):
                    act_turn(act, 0, half)
                for i in range(3):
                    act_project(act, 0, i)
                act_v(act, 0)
                act_strips(act, 0)
                act_max_copy(act, 0)

            @block.vector
            def _(dve):
                dve.wait_ge(s_x, 16)
                for half in (0, 1):
                    dve_norm(dve, 0, half)
                for half in (0, 1):
                    dve_turn(dve, 0, half)
                for i in range(3):
                    dve_project(dve, 0, i)
                for i in range(PACKS):
                    dve_maxima(dve, 0, i)

            @block.gpsimd
            def _(pool):
                for half in (0, 1):
                    pool_norm(pool, 0, half)
                for i in range(3):
                    pool_project(pool, 0, i)

        nc.all_engine_barrier()
        clear_all()
        nc.all_engine_barrier()

        with nc.Fori(0, B) as b:
            with nc.Block() as block:
                @block.sync
                def _(sp):
                    def rest_of_unit(u):
                        for j in (TILE_IN.get(u), TILE_AFTER.get(u)):
                            if j is not None and UP_SLOTS <= j + 2 < J_ALL:
                                up_load(sp, j + 2)
                        if not last_of_layer(u) and not last_of_layer(u + 1):
                            sp.wait_ge(s_sc, PACKS * (u + 1))
                            ring_load(sp, u + 2)
                        if not last_of_layer(u):
                            max_row(sp, u + 1)

                    for u in range(UNITS[0]):
                        rest_of_unit(u)
                    up_load(sp, FRONT_TILES[0] + 2)
                    write_images(sp, 1, (0, 1))
                    ring_load(sp, UNITS[0])
                    ring_load(sp, UNITS[0] + 1)
                    write_images(sp, 1, (2, 3))
                    for j in FRONT_TILES[1:-1]:
                        up_load(sp, j + 2)
                    max_row(sp, UNITS[0])
                    up_load(sp, FRONT_TILES[-1] + 2)
                    load_x(sp, bass.ds((b + 1) * T, T))
                    for u in range(UNITS[0], U_ALL):
                        rest_of_unit(u)
                    sp.wait_ge(s_u, J_ALL)
                    for j in range(UP_SLOTS):
                        sp.dma_start(upring[:, j].rearrange("p a h k n -> p (a h k n)").bitcast(F32), up_img[j])\
                            .then_inc(s_uppre, 16)
                    write_images(sp, 0, range(3))
                    ring_load(sp, 0)
                    ring_load(sp, 1)
                    max_row(sp, 0)
                    sp.wait_ge(s_xr, 4)
                    sp.dma_start(out[bass.ts(b, T), :].rearrange("(t p) c -> p t c", p=P), x[:]).then_inc(s_out, 16)
                    wait_images(sp, 0, 3)
                    sp.wait_ge(s_ring[1], 32)
                    sp.wait_ge(s_uppre, 16 * UP_SLOTS)
                    sp.wait_ge(s_mrow[0], 16)
                    sp.wait_ge(s_out, 16)

                @block.tensor
                def _(pe):
                    def unit(u):
                        more = not last_of_layer(u)
                        if more:
                            wait_ring(pe, u + 1)
                        for i in range(PACKS):
                            pe_score_pack(pe, u, i)
                            if more:
                                pe_max_pack(pe, u + 1, i)
                            if u in TILE_IN:
                                pe_up_between(pe, TILE_IN[u], i)
                            if i == 2 and u not in U0:
                                pe_out_turn(pe, u - 1)
                            if i == 5:
                                pe_pv(pe, u, 0)
                            if u == U_ALL - 1 and i in (3, 7):
                                pe_turn(pe, 0, (3, 7).index(i))
                        pe_pv(pe, u, 1)
                        if more:
                            if u:
                                pe.wait_ge(s_on, u)
                            pe_max_turn(pe, u + 1)
                        pe_up(pe, TILE_AFTER[u], 0)
                        pe_pv(pe, u, 2)
                        pe_up(pe, TILE_AFTER[u], 1)
                        pe_pv(pe, u, 3)
                        if u == UNITS[0] - 1:
                            pe_out_turn(pe, u)

                    for u in range(UNITS[0]):
                        unit(u)
                    pe_down(pe, 0, 0)
                    pe_down(pe, 0, 1)
                    pe_o_turn(pe, 0)
                    pe_attention_out(pe, 0, 0)
                    pe_down(pe, 0, 2)
                    pe_down(pe, 0, 3)
                    pe_turn(pe, 1, 0)
                    pe_attention_out(pe, 0, 1)
                    pe_turn(pe, 1, 1)
                    pe.wait_ge(s_xnlo[1], 2 * KC)
                    pe_project(pe, 1, 0)
                    pe_project(pe, 1, 1)
                    pe_v(pe, 1)
                    pe_project(pe, 1, 2)
                    pe_project(pe, 1, 3)
                    pe.wait_ge(s_v[1], 1)
                    for tt in range(NT):
                        last = product(MISC[:, tt * NE:(tt + 1) * NE], xnT[1], wgate,
                                       lambda t, p, k: t[:, p, k, tt * P:(tt + 1) * P], lambda w, p, k: w[:, p, k, :])
                    last.then_inc(s_rp, 1)
                    for j in FRONT_TILES[:2]:
                        pe_up(pe, j, 0)
                        pe_up(pe, j, 1)
                    pe.wait_ge(s_rtk, 9)
                    for tt in range(NT):
                        last = nc.tensor.transpose(MISC[0:NE, tt * P:(tt + 1) * P], rt[:, 4, tt, :], ident[:])
                    last.then_inc(s_rT, 1)
                    pe.wait_ge(s_pc[1], 4)
                    wait_ring(pe, UNITS[0])
                    for i in range(PACKS):
                        pe_max_pack(pe, UNITS[0], i)
                        if i in (2, 4):
                            pe_up(pe, FRONT_TILES[2], (2, 4).index(i))
                        if i in (6, 8):
                            pe_up(pe, FRONT_TILES[3], (6, 8).index(i))
                    pe.wait_ge(s_rTc, 1)
                    pe_max_turn(pe, UNITS[0])
                    pe_up(pe, FRONT_TILES[4], 0)
                    pe_up(pe, FRONT_TILES[4], 1)
                    for u in range(UNITS[0], U_ALL):
                        unit(u)
                    pe.wait_ge(s_xnlo[0], 2 * KC)
                    for i in range(3):
                        pe_project(pe, 0, i)
                    pe_v(pe, 0)
                    pe_out_turn(pe, U_ALL - 1)
                    pe_down(pe, 1, 0)
                    pe_down(pe, 1, 1)
                    wait_ring(pe, 0)
                    pe.wait_ge(s_v[0], 1)
                    work = [(tt, j) for tt in (2, 3) for j in range(HT[1])]
                    done = 0
                    for i in range(PACKS):
                        pe_max_pack(pe, 0, i)
                        upto = len(work) * (i + 1) // PACKS
                        for tt, j in work[done:upto]:
                            pe_down(pe, 1, tt, [j])
                        done = upto
                    pe_o_turn(pe, 1)
                    pe_attention_out(pe, 1, 0)
                    pe_attention_out(pe, 1, 1)
                    pe_max_turn(pe, 0)

                @block.scalar
                def _(act):
                    def unit(u):
                        for i in range(PACKS):
                            act_exps(act, u, i)
                            if i == 1 and u not in U0:
                                act_pv_copy(act, u - 1)
                            if i == 6 and u in TILE_IN:
                                act_tanh(act, TILE_IN[u])
                            if u == U_ALL - 1 and i in (5, 9):
                                act_turn(act, 0, (5, 9).index(i))
                        if not last_of_layer(u):
                            act_max_copy(act, u + 1)
                        act_tanh(act, TILE_AFTER[u])
                        if u < UNITS[0] - 1:
                            act.wait_ge(s_pm, 4 * u + 4)
                            act.wait_ge(s_pm3, 4 * u + 4)
                            act_strips(act, u + 1)
                        if last_of_layer(u):
                            act_pv_copy(act, u)

                    for u in range(UNITS[0]):
                        unit(u)
                    act_tanh_down(act, 0, 0)
                    act_o_turn(act, 0)
                    act_tanh_down(act, 0, 1)
                    act_turn(act, 1, 0)
                    act_turn(act, 1, 1)
                    act_project(act, 1, 0)
                    act_project(act, 1, 1)
                    act_v(act, 1)
                    act_project(act, 1, 2)
                    act_project(act, 1, 3)
                    act.wait_ge(s_rp, 1)
                    nc.scalar.activation(rt[:, 0].rearrange("p t e -> p (t e)"), MISC[:, 0:NT * NE], ACT.Tanh,
                                         scale=0.5).then_inc(s_rsg, 1)
                    for j in FRONT_TILES[:2]:
                        act_tanh(act, j)
                    act.wait_ge(s_rT, 1)
                    nc.scalar.copy(gT[:], MISC[0:NE, :]).then_inc(s_rTc, 1)
                    for j in FRONT_TILES[2:4]:
                        act_tanh(act, j)
                    act_max_copy(act, UNITS[0])
                    act_tanh(act, FRONT_TILES[4])
                    for u in range(UNITS[0], U_ALL):
                        unit(u)
                    for i in range(3):
                        act_project(act, 0, i)
                    act_v(act, 0)
                    act.wait_ge(s_rm, 1)
                    act_strips(act, 0)
                    act_tanh_down(act, 1, 0)
                    act_tanh_down(act, 1, 1)
                    act_o_turn(act, 1)
                    act.wait_ge(s_mrow[1], 16 * (U_ALL - 1))
                    act_max_copy(act, 0)

                @block.vector
                def _(dve):
                    def unit(u):
                        more = not last_of_layer(u)
                        for i in range(PACKS):
                            if more:
                                dve_maxima(dve, u + 1, i)
                            if layer_of(u) == 0 and i in (4, 8, 10):
                                dve_distances(dve, u, (4, 8, 10).index(i))
                            if i == 0 and u not in U0:
                                dve_linear_half(dve, TILE_AFTER[u - 1])
                            if i == 4 and u not in U0:
                                dve_normalise(dve, u - 1)
                            if u in TILE_IN and i == 7:
                                dve_gate_half(dve, TILE_IN[u])
                        if u in TILE_IN:
                            dve_linear_half(dve, TILE_IN[u])
                        if layer_of(u) == 0:
                            dve_distances(dve, u, 3)
                        dve_gate_half(dve, TILE_AFTER[u])
                        if last_of_layer(u):
                            dve_linear_half(dve, TILE_AFTER[u])
                            if u < U_ALL - 1:
                                dve_normalise(dve, u)

                    for u in range(UNITS[0]):
                        unit(u)
                    dve_down_half(dve, 0, 0)
                    dve_update_x(dve, 0, 0)
                    dve_norm(dve, 1, 0)
                    dve_down_half(dve, 0, 1)
                    dve_turn(dve, 1, 0)
                    dve_update_x(dve, 0, 1)
                    dve_norm(dve, 1, 1)
                    dve_turn(dve, 1, 1)
                    for i in range(4):
                        dve_project(dve, 1, i)
                    dve_gate_half(dve, FRONT_TILES[0])
                    dve_linear_half(dve, FRONT_TILES[0])
                    dve_router(dve)
                    dve_gate_half(dve, FRONT_TILES[1])
                    dve_linear_half(dve, FRONT_TILES[1])
                    for i in range(PACKS):
                        dve_maxima(dve, UNITS[0], i)
                        if i == 4:
                            dve_gate_half(dve, FRONT_TILES[2])
                        if i == 6:
                            dve_linear_half(dve, FRONT_TILES[2])
                        if i == 8:
                            dve_gate_half(dve, FRONT_TILES[3])
                    dve_linear_half(dve, FRONT_TILES[3])
                    dve_gate_half(dve, FRONT_TILES[4])
                    dve_linear_half(dve, FRONT_TILES[4])
                    for u in range(UNITS[0], U_ALL - 1):
                        unit(u)
                    dve_linear_half(dve, TILE_AFTER[U_ALL - 2])
                    dve.wait_ge(s_x, 16)
                    for half in (0, 1):
                        dve_norm(dve, 0, half)
                    dve_normalise(dve, U_ALL - 2)
                    for half in (0, 1):
                        dve_turn(dve, 0, half)
                    dve_gate_half(dve, TILE_AFTER[U_ALL - 1])
                    dve_linear_half(dve, TILE_AFTER[U_ALL - 1])
                    for i in range(3):
                        dve_project(dve, 0, i)
                    dve_normalise(dve, U_ALL - 1)
                    dve_rms(dve)
                    dve_down_half(dve, 1, 0)
                    dve.wait_ge(s_mT[1], U_ALL - 2)
                    for i in range(PACKS):
                        dve_maxima(dve, 0, i)
                    dve_down_half(dve, 1, 1)
                    dve_update_x(dve, 1, 0)
                    dve_update_x(dve, 1, 1)

                def weigh(pool, j):
                    n = j - HT[0] - SHARED_T
                    if n < 0:
                        return
                    pool.wait_ge(s_h, j + 1)
                    pool.wait_ge(s_gr[n % 2], 16 * sum(len(gate_segments(m)) for m in range(n % 2, n + 1, 2)))
                    h = hbuf[:, j - HT[0], :]
                    nc.gpsimd.tensor_tensor(h, h, gring[:, n % 2, :], ALU.mult).then_inc(s_hw, 1)

                def gate_load(pool, j):
                    n = j - HT[0] - SHARED_T
                    if n < 0 or j >= J_ALL:
                        return
                    if n >= 2:
                        pool.wait_ge(s_hw, n - 1)
                    for e, r, m in gate_segments(n):
                        nc.gpsimd.dma_start(gring[r:r + m, n % 2, :],
                                            gate_img[e].partition_broadcast(m)).then_inc(s_gr[n % 2], 16)

                @block.gpsimd
                def _(pool):
                    for u in range(UNITS[0]):
                        for kt in range(NT):
                            pool_distances(pool, u, kt)
                    for half in (0, 1):
                        pool_norm(pool, 1, half)
                    for i in range(4):
                        pool_project(pool, 1, i)
                    pool.wait_ge(s_rTc, 1)
                    nc.gpsimd.dma_start(gate_img, gT[:]).then_inc(s_rimg, 16)
                    pool.wait_ge(s_rimg, 16)
                    first = HT[0] + SHARED_T
                    gate_load(pool, first)
                    gate_load(pool, first + 1)
                    for j in FRONT_TILES:
                        if j >= first:
                            weigh(pool, j)
                            gate_load(pool, j + 2)
                    for u in range(UNITS[0], U_ALL):
                        if u == U_ALL - 1:
                            for half in (0, 1):
                                pool_norm(pool, 0, half)
                        for kt in range(NT):
                            pool.wait_ge(s_exp, PACKS * u + PACKS_TO[kt])
                            pr = probs[:, kt % 2, :, 0:P]
                            nc.gpsimd.affine_select(pr, pr, [[0, G4], [1, P]], ALU.is_ge, 0.0, base=0,
                                                    channel_multiplier=-1).then_inc(s_pm, 1)
                            if kt == 0 and u - 1 in TILE_AFTER and u > UNITS[0]:
                                weigh(pool, TILE_AFTER[u - 1])
                                gate_load(pool, TILE_AFTER[u - 1] + 2)
                        if u in TILE_IN:
                            weigh(pool, TILE_IN[u])
                            gate_load(pool, TILE_IN[u] + 2)
                    weigh(pool, TILE_AFTER[U_ALL - 1])
                    for i in range(3):
                        pool_project(pool, 0, i)

            nc.gpsimd.dma_reset()
            nc.all_engine_barrier()
            clear_all()
            nc.all_engine_barrier()


def kernel(**inputs):
    import numpy as np
    import concourse.bacc as bacc
    from concourse.bass_utils import run_bass_kernel_spmd

    a = {k: np.asarray(v) for k, v in inputs.items()}

    def chunks(w):
        return np.ascontiguousarray(w.T.reshape(KC, P, -1).transpose(1, 0, 2))

    def up_tiles(gate, lin):
        both = np.stack([gate, lin]).reshape(2, -1, P, KC, P)
        return both.transpose(1, 4, 0, 3, 2).reshape(-1, P, 2 * KC * P)

    def down_tiles(w):
        return np.ascontiguousarray(w.T.reshape(-1, P, C).transpose(1, 0, 2))

    hs = 352
    pad = np.zeros((SHARED_T * P - hs, C), np.float32)
    gw, up, dn = a["L1_ffn_shared_gw"], a["L1_ffn_up_w"], a["L1_ffn_down_w"]
    gate1 = np.concatenate([gw[hs:], pad, up[:, :EH].reshape(-1, C)])
    lin1 = np.concatenate([gw[:hs], pad, up[:, EH:].reshape(-1, C)])
    down1 = np.concatenate([a["L1_ffn_shared_dw"], pad.T, dn.transpose(1, 0, 2).reshape(C, -1)], axis=1)

    had = np.ones((1, 1), np.float32)
    while had.shape[0] < P:
        had = np.block([[had, had], [had, -had]])
    d = np.arange(T)[None, :] - np.arange(P)[:, None]
    dist = np.where(d >= 0, np.sqrt(np.maximum(d, 0)), 1.0e30).astype(np.float32)
    causal = np.where(np.arange(P)[None, :] <= np.arange(P)[:, None], 0.0, -BIG).astype(np.float32)
    xs = a["L0_attn_x"]
    arrays = {
        "x": np.concatenate([xs, xs[-1:]]).reshape(-1, C),
        "w0_qk": chunks(np.concatenate([a["L0_attn_Wq"], a["L0_attn_Wk"]])),
        "w0_v": chunks(a["L0_attn_Wv"]),
        "w0_o": chunks(a["L0_attn_Wo"]),
        "w_up": np.concatenate([up_tiles(a["L0_ffn_W1"], a["L0_ffn_W3"]), up_tiles(gate1, lin1)]),
        "w0_down": down_tiles(a["L0_ffn_W2"]),
        "w1_qk": chunks(np.concatenate([a["L1_attn_Wq"], a["L1_attn_Wk"]])),
        "w1_v": chunks(a["L1_attn_Wv"]),
        "w1_o": chunks(a["L1_attn_Wo"]),
        "w1_down": down_tiles(down1),
        "w1_gate": chunks(a["L1_ffn_gate_w"]),
        "gate_bias": a["L1_ffn_gate_bias"],
        "lambdas": np.concatenate([a[f"L1_attn_lambda_{n}"] for n in ("q1", "k1", "q2", "k2")]),
        "subln": a["L1_attn_subln_weight"],
        "c_ident": np.eye(P, dtype=np.float32),
        "c_hadamard": (had / 32).astype(np.float32),
        "c_dist": dist,
        "c_causal": causal,
    }
    nc = bacc.Bacc("TRN2", target_bir_lowering=False, num_devices=1)
    args = [nc.dram_tensor("in_" + n, v.shape, mybir.dt.from_np(v.dtype), kind="ExternalInput").ap()
            for n, v in arrays.items()]
    out = nc.dram_tensor("out", (B * T, C), F32, kind="ExternalOutput").ap()
    gated_layers_kernel(nc, *args, out)
    r = run_bass_kernel_spmd(nc, [{"in_" + n: v for n, v in arrays.items()}], core_ids=[0])
    return r.results[0]["out"].reshape(B, T, C)
```

```python
import math
from contextlib import ExitStack

import concourse.bass as bass
from concourse import mybir

F32 = mybir.dt.float32
F32R = mybir.dt.float32r
BF16 = mybir.dt.bfloat16
I32 = mybir.dt.int32
ALU = mybir.AluOpType
ACT = mybir.ActivationFunctionType
AX = mybir.AxisListType

P = 128
T = 512
NT = T // P
C = 256
KC = C // P
B = 8
G4 = 4
UNITS = (4, 8)
U0 = (0, UNITS[0])
U_ALL = sum(UNITS)
DH = (16, 8)
DV = 16
NV = (4, 16)
ROWS = (48, 32)
EXP_SCALE = (1.0 / math.sqrt(16), 1.0 / math.sqrt(8))
HT = (8, 14)
J_ALL = sum(HT)
SHARED_T = 3
NE = 8
EH = 176
EPS = 1e-5
LAMBDA_INIT = 0.8 - 0.6 * math.exp(-0.3 * 12)
BIG = 3.0e38
QK_MAX = 1.0e18
RSQRT_MAGIC = 1597463007.0
MROW = P - 1
PACKS = 11
SCORE_PACKS = [(0, g, 1) for g in range(4)] + [(1, g, 1) for g in range(4)] + [(2, 0, 2), (2, 2, 2), (3, 0, 4)]
MAX_PACKS = [(3, g, 1) for g in range(4)] + [(2, g, 1) for g in range(4)] + [(1, 0, 2), (1, 2, 2), (0, 0, 4)]
PACKS_TO = (4, 8, 10, 11)
SLOPES = [float((2.0 ** -0.5) ** (h + 1)) for h in range(16)]
TILE_IN = {1: 2, 2: 4, 3: 6}
TILE_AFTER = {0: 1, 1: 3, 2: 5, 3: 7, 4: 14, 5: 15, 6: 16, 7: 17, 8: 18, 9: 19, 10: 20, 11: 21}
FRONT_TILES = (8, 9, 10, 11, 12, 13)
UP_SLOTS = 3
UP_EARLY = 8
RMS_STEPS = 17
PROJ = [
    [(True, 0, 128, 0), (False, 256, 64, 0), (True, 128, 128, 8)],
    [(True, 0, 128, 0), (False, 256, 128, 0), (True, 128, 128, 16), (False, 384, 128, 16)],
]
PASSES = ((0, 0), (0, 1), (1, 0))
UP_STEPS = KC * len(PASSES)


def layer_of(u):
    return 0 if u < UNITS[0] else 1


def last_of_layer(u):
    return u in (UNITS[0] - 1, U_ALL - 1)


def layer_tile(j):
    return (0, j) if j < HT[0] else (1, j - HT[0])


def gate_segments(n):
    r, out = P * n, []
    while r < P * n + P:
        e = r // EH
        m = min(EH * (e + 1), P * n + P) - r
        out.append((e, r - P * n, m))
        r += m
    return out


def gated_layers_kernel(nc, x_in, w0_qk, w0_v, w0_o, w_up, w0_down, w1_qk, w1_v, w1_o, w1_down,
                        w1_gate, gate_bias, lambdas, subln, c_ident, c_hadamard, c_dist, c_causal, out):
    with ExitStack() as ctx:
        def sb(name, shape, dt=F32):
            return ctx.enter_context(nc.sbuf_tensor(name, shape, dt))

        def sem(name):
            s = ctx.enter_context(nc.semaphore(name))
            body_sems.append(s)
            return s

        def clear(sems):
            first, last = sems[0].num, sems[-1].num
            assert last - first + 1 == len(sems)
            nc.sync.sem_clear(range(first, last + 1))

        body_sems = []
        dram = lambda name, shape: nc.dram_tensor(name, shape, F32, kind="Internal").ap()
        q_img = [dram(f"q_img{l}", [UNITS[l] * G4, ROWS[l], T]) for l in (0, 1)]
        k_img = [dram("k_img0", [4, ROWS[0], T]), dram("k_img1", [32, ROWS[1], T])]
        gate_img = dram("gate_img", [NE, T])
        up_img = dram("up_img", [J_ALL, P, 2 * T])

        wqk = [sb("wqk0", [P, 2, KC, 320], F32R), sb("wqk1", [P, 2, KC, 512], F32R)]
        wv = [sb("wv0", [P, 2, KC, 64], F32R), sb("wv1", [P, 2, KC, 256], F32R)]
        wgate = sb("wgate", [P, 2, KC, NE], F32R)
        wo = [sb("wo0", [P, KC, C]), sb("wo1", [P, KC, C])]
        wdown = [sb("wdown0", [P, HT[0], C]), sb("wdown1", [P, HT[1], C])]
        bias_e = sb("bias_e", [P, NE])
        lam_in = sb("lam_in", [P, 4, 8])
        lam = sb("lam", [P, 8])
        gln = sb("gln", [P, DV])
        ident = sb("ident", [P, P])
        ident_bf = sb("ident_bf", [P, P], BF16)
        causal_bf = sb("causal_bf", [P, G4, P], BF16)
        dist = sb("dist", [P, T])
        minus_half = sb("minus_half", [P, 4])
        qring = [sb("qring0", [P, 2, G4, T], F32R), sb("qring1", [P, 2, G4, T], F32R)]
        kring = [sb("kring0", [P, 2, T], F32R), sb("kring1", [P, 2, T], F32R)]
        upring = sb("upring", [P, UP_SLOTS, 2, 2, KC, P], F32R)
        gring = sb("gring", [P, 2, T])
        hbuf = sb("hbuf", [P, HT[1], T])
        probs = sb("probs", [P, 2, G4, T])
        slots = probs[:].rearrange("p a g n -> p (a g) n")
        xin = sb("xin", [P, NT, C])
        x = sb("x", [P, NT, C])
        xn = [sb("xn0", [P, NT, C]), sb("xn1", [P, NT, C])]
        xnT = [sb("xnT0", [P, 2, KC, T], F32R), sb("xnT1", [P, 2, KC, T], F32R)]
        v = [sb("v0", [P, NT, NV[0], DV + 1]), sb("v1", [P, NT, NV[1], DV + 1])]
        shared8 = sb("shared8", [P, 2048])
        estrip = shared8[:].rearrange("p (g n) -> p g n", g=G4)
        on = shared8[:].rearrange("p (t h d) -> p t h d", t=NT, h=32)
        o_sb = xn
        oT = slots[:, 6:8, :]
        ot = sb("ot", [P, T])
        tb = sb("tb", [P, T])
        fo = sb("fo", [P, NT, C])
        stats = sb("stats", [P, NT, 6])
        mv = sb("mv", [P, NT, 2])
        rstd = sb("rstd", [P, NT])
        rden = sb("rden", [P, 16])
        nmax = sb("nmax", [P, 2, G4, NT])
        mneg = sb("mneg", [G4 * NT, P], F32R)
        rt = sb("rt", [P, 6, NT, NE])
        rs = sb("rs", [P, NT])
        gT = sb("gT", [NE, T])
        nw = sb("nw", [P, 4, 64])

        bank = [ctx.enter_context(nc.psum_tensor(f"bank{i}", [P, 512], F32)) for i in range(8)]
        MX, SC, PV, MISC, FB = bank[0:2], bank[2:4], bank[4], bank[5], bank[6:8]

        s_zero = sem("zeros_and_ones_ready")
        s_v0 = sem("v_ones_ready")
        s_qz = sem("rings_zeroed")
        s_pad = sem("image_padding_written")
        s_ones = sem("image_ones_written")
        s_kones = sem("ring_ones_written")
        s_uin = [sem(f"up_weights_in_{i}") for i in range(4)]
        s_uhi = sem("up_weights_high")
        s_ulo = sem("up_weights_low")
        s_uout = [sem(f"up_weights_out_{i}") for i in range(4)]
        s_raw = sem("raw_weights_loaded")
        s_rhi = sem("weights_high")
        s_rlo = sem("weights_low")
        s_wd = sem("down_weights_loaded")
        s_small = sem("constants_loaded")
        s_mask = sem("masks_ready")
        s_big = sem("other_weights_loaded")
        s_fw = sem("butterflies_done")
        s_had = sem("hadamard_products_ready")
        s_hade = sem("hadamard_products_copied")
        s_lam = sem("lambda_steps")
        s_lamx = sem("lambda_exps")
        tmp8 = hbuf[:, 8:12, :].rearrange("p a n -> p (a n)").rearrange("p (t n) -> p t n", t=HT[0])
        zero_t = hbuf[:, 12:14, :]
        ones_row = ot[:]
        hadamard = tb[:, 0:P]
        causal_f = tb[:, P:2 * P]
        n_ustage = 4
        raw = [(slots[:, 0:2, :].rearrange("p a n -> p (a n)")[:, 0:640], wqk[0], w0_qk),
               (slots[:, 2:4, :].rearrange("p a n -> p (a n)")[:, 0:1024], wqk[1], w1_qk),
               (slots[:, 4, 0:128], wv[0], w0_v), (slots[:, 5, 0:512], wv[1], w1_v), (slots[:, 6, 0:16], wgate, w1_gate)]
        setup_sems, body_sems = body_sems, []

        two = lambda name: [sem(f"{name}_{l}") for l in (0, 1)]
        s_x = sem("x_loaded")
        s_stat, s_aggr, s_veps, s_rstd = two("stats_ready"), two("moments_ready"), two("var_plus_eps"), two("rstd_ready")
        s_xn, s_xnTp, s_xnhi, s_xnlo = two("xn_ready"), two("xnT_in_psum"), two("xnT_high_ready"), two("xnT_low_ready")
        s_proj, s_pc = two("projection_in_psum"), two("projection_copied")
        s_phi, s_plo = two("projection_high_ready"), two("projection_low_ready")
        s_img = [[sem(f"image_written_{l}_{i}") for i in range(len(PROJ[l]))] for l in (0, 1)]
        s_vp, s_v = two("v_in_psum"), two("v_ready")
        s_rp = sem("router_logits_in_psum")
        s_rtk = sem("router_steps")
        s_rsg = sem("router_tanh_ready")
        s_rT = sem("router_weights_transposed")
        s_rTc = sem("router_weights_copied")
        s_rimg = sem("router_weights_written")
        s_mp, s_mr, s_mT = two("max_scores_in_psum"), two("max_reduced"), two("max_transposed")
        s_mc, s_mrow = two("max_copied"), two("max_row_loaded")
        s_ring = {u: sem(f"ring_of_unit_{u}_loaded") for u in (0, 1)}
        s_ringn = [sem("ring_even_loaded"), sem("ring_odd_loaded")]
        s_sc = sem("scores_in_psum")
        s_exp = sem("exps_ready")
        s_es = sem("distance_factors_ready")
        s_pm = sem("probs_masked")
        s_pc2 = sem("pool_heads_probs_causal")
        s_pm2 = sem("pool_heads_probs_masked")
        s_pv = sem("pv_done")
        s_ot = sem("pv_copied")
        s_oTp = sem("outputs_transposed")
        s_rd = sem("denominators_inverted")
        s_on = sem("outputs_normalised")
        s_up = [sem(f"up_weights_loaded_{i}") for i in range(UP_SLOTS)]
        s_uppre = [sem(f"next_up_weights_loaded_{i}") for i in range(UP_SLOTS)]
        s_gr = [sem("expert_weights_loaded_even"), sem("expert_weights_loaded_odd")]
        s_g = sem("gate_half_in_psum")
        s_u = sem("linear_half_in_psum")
        s_t = sem("tanh_ready")
        s_gu = sem("gate_half_used")
        s_h = sem("hidden_ready")
        s_hw = sem("hidden_weighted")
        s_dn = sem("down_in_psum")
        s_fo = sem("ffn_silu_ready")
        s_rm = sem("rms_steps")
        s_oTt = sem("o_transposed_in_psum")
        s_oTs = sem("oT_ready")
        s_so = sem("attention_out_in_psum")
        s_gx = sem("gated_ready")
        s_xr = sem("x_updated")
        s_out = sem("out_written")

        def stage(i, part):
            return slots[:, 2 * i + part, :]

        def wait_images(eng, l, tiles):
            for i in range(tiles):
                eng.wait_ge(s_img[l][i], 48)

        def mx(u):
            return (0, 0) if u == 0 else (1, u - 1)

        def load_x(sp, t0):
            sp.dma_start(xin[:], x_in[t0, :].rearrange("(t p) c -> p t c", p=P)).then_inc(s_x, 16)

        def write_images(sp, l, tiles):
            for i in tiles:
                is_q, _, m, h0 = PROJ[l][i]
                d = DH[l]
                img = (q_img if is_q else k_img)[l][h0:h0 + m // d]
                sp.wait_ge(s_phi[l], i + 1)
                for t, part in ((0, 0), (1, 0), (2, 1)) if is_q else ((0, 0), (2, 0), (1, 1)):
                    if part:
                        sp.wait_ge(s_plo[l], i + 1)
                    sp.dma_start(img[:, d * t:d * t + d, :], stage(i, part)[0:m, :]).then_inc(s_img[l][i], 16)

        def ring_load(sp, u):
            l = layer_of(u)
            w = u - U0[l]
            s = u % 2
            done = s_ring[u] if u < 2 else s_ringn[s]
            if l == 0:
                if w < 2:
                    wait_images(sp, 0, 2)
                sp.dma_start(qring[0][0:48, s, :, :].bitcast(F32),
                             q_img[0][4 * w:4 * w + 4].rearrange("g r n -> r g n")).then_inc(done, 16)
                sp.dma_start(kring[0][0:48, s, :].bitcast(F32), k_img[0][w]).then_inc(done, 16)
            else:
                wait_images(sp, 1, 2 if w < 4 else 4)
                for g in range(G4):
                    sp.dma_start(qring[1][32 * g:32 * g + 32, s, g, :].bitcast(F32), q_img[1][4 * w + g]).then_inc(done, 16)
                sp.dma_start(kring[1][:, s, :].bitcast(F32),
                             k_img[1][4 * w:4 * w + 4].rearrange("g r n -> (g r) n")).then_inc(done, 16)

        def wait_ring(eng, u):
            if u == 0:
                eng.wait_ge(s_ring[0], 32)
            elif u >= 2:
                eng.wait_ge(s_ringn[u % 2], 16 * sum(2 if layer_of(i) == 0 else 5 for i in range(2 + u % 2, u + 1, 2)))

        def max_row(sp, u):
            k, n = mx(u)
            sp.wait_ge(s_mc[k], n + 1)
            sp.dma_start(qring[layer_of(u)][MROW:MROW + 1, u % 2, :, :].rearrange("a g (t n) -> a (g t) n", t=NT)
                         .bitcast(F32), mneg[:].bitcast(F32)).then_inc(s_mrow[k], 16)

        def up_load(sp, j, done=None):
            if j > UP_SLOTS:
                sp.wait_ge(s_u, j - UP_SLOTS)
            sp.dma_start(upring[:, j % UP_SLOTS].rearrange("p a h k n -> p (a h k n)").bitcast(F32), up_img[j])\
                .then_inc(done or s_up[j % UP_SLOTS], 16)

        def product(out_ap, a, b, part_a, part_b, first=0, count=KC * len(PASSES)):
            steps = [(k, pa, pb) for k in range(KC) for pa, pb in PASSES]
            for n in range(first, first + count):
                k, pa, pb = steps[n]
                last = nc.tensor.matmul(out_ap, part_a(a, pa, k), part_b(b, pb, k), start=(n == 0),
                                        stop=(n == len(steps) - 1))
            return last

        def pe_turn(pe, l, half):
            pe.wait_ge(s_xn[l], half + 1)
            if half:
                pe.wait_ge(s_xnlo[l], KC)
            for k in range(KC):
                for tt in (2 * half, 2 * half + 1):
                    last = nc.tensor.transpose(MX[k][:, tt * P:(tt + 1) * P], xn[l][:, tt, k * P:(k + 1) * P], ident[:])
            last.then_inc(s_xnTp[l], 1)

        def token_half(half):
            return slice(0, T) if half is None else slice(half * T // 2, (half + 1) * T // 2)

        def pe_project(pe, l, i, half=None):
            _, c0, m, _ = PROJ[l][i]
            cols = token_half(half)
            if l == 0 and i == 2:
                pe.wait_ge(s_pc[0], 1)
            bk = [[MX[0], MX[1], MX[0]], [SC[0], SC[1], MX[0], MX[1]]][l][i]
            last = product(bk[0:m, cols], wqk[l], xnT[l], lambda w, p, k: w[:, p, k, c0:c0 + m],
                           lambda t, p, k: t[:, p, k, cols])
            if half != 0:
                last.then_inc(s_proj[l], 1)

        def pe_v(pe, l, tts=range(NT)):
            w = DV * NV[l]
            if l == 0:
                pe.wait_ge(s_pc[0], 2)
            for tt in tts:
                o = MX[1][:, tt * w:(tt + 1) * w] if l == 0 else (PV, MISC)[tt // 2][:, (tt % 2) * w:(tt % 2 + 1) * w]
                last = product(o, xnT[l], wv[l], lambda t, p, k: t[:, p, k, tt * P:(tt + 1) * P],
                               lambda w_, p, k: w_[:, p, k, :])
            if tt == NT - 1:
                last.then_inc(s_vp[l], 1)

        def pe_max_pack(pe, u, i):
            l, s = layer_of(u), u % 2
            k, before = mx(u)
            n = PACKS * before + i
            qt, g0, heads = MAX_PACKS[i]
            w = P * (qt + 1)
            if n >= 2:
                pe.wait_ge(s_mr[k], n - 1)
            bk = MX[n % 2]
            for g in range(g0, g0 + heads):
                nc.tensor.matmul(bk[:, (g - g0) * w:(g - g0 + 1) * w], qring[l][0:MROW, s, g, qt * P:(qt + 1) * P],
                                 kring[l][0:MROW, s, 0:w], start=True, stop=True)
            diag = bk[:, 0:heads * w].rearrange("p (g n) -> p g n", g=heads)[:, :, qt * P:w]
            nc.tensor.matmul(diag, ident_bf[:], causal_bf[:, 0:heads, :], start=False, stop=True,
                             skip_group_check=True).then_inc(s_mp[k], 1)

        def pe_max_turn(pe, u):
            k, n = mx(u)
            pe.wait_ge(s_mr[k], PACKS * (n + 1))
            nc.tensor.transpose(MISC[0:G4 * NT, 0:P], nmax[:, u % 2].rearrange("p g t -> p (g t)"), ident[:])\
                .then_inc(s_mT[k], 1)

        def pe_score_pack(pe, u, i):
            l, s = layer_of(u), u % 2
            n = PACKS * u + i
            kt, g0, heads = SCORE_PACKS[i]
            w = T - P * kt
            if n >= 2:
                pe.wait_ge(s_exp, n - 1)
            if i == 0 and u:
                pe.wait_ge(s_mrow[1], 16 * u)
            nc.tensor.matmul(SC[n % 2][:, 0:heads * w].rearrange("p (g n) -> p g n", g=heads),
                             kring[l][:, s, kt * P:(kt + 1) * P],
                             qring[l][:, s, g0:g0 + heads, kt * P:T], start=True, stop=True).then_inc(s_sc, 1)

        def pe_pv(pe, u, kt):
            l = layer_of(u)
            if l == 0:
                pe.wait_ge(s_pm, 2 * (4 * u + kt + 1))
                pe.wait_ge(s_pm2, 4 * u + kt + 1)
            else:
                pe.wait_ge(s_pm, 8 * U0[1] + 4 * (u - U0[1]) + kt + 1)
            if kt == 0 and u:
                pe.wait_ge(s_ot, u)
            for g in range(G4):
                hv = u if l == 0 else 2 * (u - U0[1]) + g // 2
                last = nc.tensor.matmul(PV[32 * g:32 * g + DV + 1, kt * P:T], v[l][:, kt, hv, :],
                                        probs[:, kt % 2, g, 0:T - P * kt], start=(kt == 0),
                                        stop=(kt == NT - 1), skip_group_check=True)
            last.then_inc(s_pv, 1)

        def pe_out_turn(pe, u):
            pe.wait_ge(s_ot, u + 1)
            if not last_of_layer(u):
                pe.wait_ge(s_mc[1], u + 1)
            else:
                pe.wait_ge(s_on, u)
            for tt in range(NT):
                last = nc.tensor.transpose(MISC[:, tt * P:(tt + 1) * P], ot[:, tt * P:(tt + 1) * P], ident[:])
            last.then_inc(s_oTp, 1)

        def pe_up(pe, j, half, first=0, count=UP_STEPS, tokens=None):
            l, _ = layer_tile(j)
            cols = token_half(tokens)
            if first == 0 and tokens != 1:
                pe.wait_ge((s_gu, s_h)[half], j)
                if j == HT[0]:
                    pe.wait_ge(s_fo, half + 1)
                if half == 0 and j >= UP_SLOTS:
                    pe.wait_ge(s_up[j % UP_SLOTS], 16 * (j // UP_SLOTS))
            last = product(FB[half][:, cols], upring, xnT[l], lambda w, p, k: w[:, j % UP_SLOTS, p, half, k, :],
                           lambda t, p, k: t[:, p, k, cols], first, count)
            if first + count == UP_STEPS and tokens != 0:
                last.then_inc((s_g, s_u)[half], 1)

        def pe_up_ahead(pe, half, first=0, count=UP_STEPS):
            product(FB[half][:], upring, xnT[0], lambda w, p, k: w[:, 0, p, half, k, :], lambda t, p, k: t[:, p, k, :],
                    first, count)

        def pe_up_between(pe, j, i, halves=2, packs=PACKS):
            for n in range(UP_STEPS * halves * i // packs, UP_STEPS * halves * (i + 1) // packs):
                pe_up(pe, j + n // (2 * UP_STEPS), n // UP_STEPS % 2, n % UP_STEPS, 1)

        def pe_router(pe, tts):
            for tt in tts:
                last = product(MX[1][:, tt * NE:(tt + 1) * NE], xnT[1], wgate,
                               lambda t, p, k: t[:, p, k, tt * P:(tt + 1) * P], lambda w, p, k: w[:, p, k, :])
            if tt == NT - 1:
                last.then_inc(s_rp, 1)

        def pe_down(pe, l, tt, part=None):
            js = range(HT[l]) if part is None else part
            for j in js:
                if tt == 0 and j == 0:
                    pe.wait_ge(s_gu, (HT[0], J_ALL)[l])
                    pe.wait_ge(s_h, (HT[0], J_ALL)[l] - 1)
                    if l == 1:
                        pe.wait_ge(s_hw, HT[1] - SHARED_T - 1)
                if tt == 0 and j == HT[l] - 1:
                    pe.wait_ge(s_h, (HT[0], J_ALL)[l])
                    if l == 1:
                        pe.wait_ge(s_hw, HT[1] - SHARED_T)
                last = nc.tensor.matmul(FB[tt // 2][:, (tt % 2) * C:(tt % 2 + 1) * C], hbuf[:, j, tt * P:(tt + 1) * P],
                                        wdown[l][:, j, :], start=(j == 0), stop=(j == HT[l] - 1))
            if tt % 2 and js[-1] == HT[l] - 1:
                last.then_inc(s_dn, 1)

        def pe_o_turn(pe, l):
            pe.wait_ge(s_on, (UNITS[0], U_ALL)[l])
            if l == 1:
                pe.wait_ge(s_rm, RMS_STEPS)
            for k in range(KC):
                for tt in range(NT):
                    last = nc.tensor.transpose((PV, MISC)[k][:, tt * P:(tt + 1) * P], o_sb[l][:, tt, k * P:(k + 1) * P],
                                               ident[:])
                last.then_inc(s_oTt, 1)

        def pe_attention_out(pe, l, half):
            pe.wait_ge(s_oTs, 2 * (l + 1))
            for tt in (2 * half, 2 * half + 1):
                for k in range(KC):
                    last = nc.tensor.matmul(SC[half][:, (tt % 2) * C:(tt % 2 + 1) * C], oT[:, k, tt * P:(tt + 1) * P],
                                            wo[l][:, k, :], start=(k == 0), stop=(k == KC - 1))
            last.then_inc(s_so, 1)

        def act_turn(act, l, half):
            for k in range(KC):
                act.wait_ge(s_xnTp[l], half + 1)
                nc.scalar.copy(xnT[l][:, 0, k, half * 256:half * 256 + 256],
                               MX[k][:, half * 256:half * 256 + 256]).then_inc(s_xnhi[l], 1)

        def act_project(act, l, i):
            m = PROJ[l][i][2]
            act.wait_ge(s_pc[l], i + 1)
            nc.scalar.copy(stage(i, 0)[0:m, :].bitcast(F32R), stage(i, 1)[0:m, :]).then_inc(s_phi[l], 1)

        def act_v(act, l):
            act.wait_ge(s_vp[l], 1)
            if l == 0:
                last = nc.scalar.copy(v[0][:, :, :, 0:DV], MX[1][:, 0:256].rearrange("p (t h d) -> p t h d", t=NT, h=4))
            else:
                for i in range(2):
                    last = nc.scalar.copy(v[1][:, 2 * i:2 * i + 2, :, 0:DV],
                                          (PV, MISC)[i][:].rearrange("p (t h d) -> p t h d", t=2, h=16))
            last.then_inc(s_v[l], 1)

        def act_strips(act, u):
            for g in range(G4):
                last = nc.scalar.activation(estrip[:, g, :], dist[:], ACT.Exp, scale=-SLOPES[4 * u + g])
                if u:
                    last.then_inc(s_es, 1)

        def act_max_copy(act, u):
            k, n = mx(u)
            act.wait_ge(s_mT[k], n + 1)
            if n:
                act.wait_ge(s_mrow[1], 16 * n)
            nc.scalar.copy(mneg[:], MISC[0:G4 * NT, 0:P]).then_inc(s_mc[k], 1)

        def act_exps(act, u, i):
            n = PACKS * u + i
            kt, g0, heads = SCORE_PACKS[i]
            w = T - P * kt
            act.wait_ge(s_sc, n + 1)
            if 4 * u + kt >= 2:
                act.wait_ge(s_pv, 4 * u + kt - 1)
            if u == U0[1] and i == 0:
                wait_images(act, 1, 4)
            nc.scalar.activation(probs[:, kt % 2, g0:g0 + heads, 0:w],
                                 SC[n % 2][:, 0:heads * w].rearrange("p (g n) -> p g n", g=heads),
                                 ACT.Exp, scale=EXP_SCALE[layer_of(u)]).then_inc(s_exp, 1)

        def act_tanh(act, j):
            if j:
                act.wait_ge(s_g, j)
                act.wait_ge(s_gu, j)
            if j == HT[0]:
                act.wait_ge(s_fo, 2)
            nc.scalar.activation(tb[:], FB[0][:], ACT.Tanh, scale=0.5).then_inc(s_t, 1)

        def act_tanh_down(act, l, half):
            act.wait_ge(s_dn, 2 * l + half + 1)
            act.wait_ge(s_gu, (HT[0], J_ALL)[l])
            if half:
                act.wait_ge(s_fo, 2 * l + half)
            nc.scalar.activation(tb[:], FB[half][:], ACT.Tanh, scale=0.5).then_inc(s_t, 1)

        def act_pv_copy(act, u):
            act.wait_ge(s_pv, 4 * (u + 1))
            if u:
                act.wait_ge(s_oTp, u)
            nc.scalar.copy(ot[:], PV[:]).then_inc(s_ot, 1)

        def act_o_turn(act, l):
            for k in range(KC):
                act.wait_ge(s_oTt, 2 * l + k + 1)
                nc.scalar.copy(oT[:, k, :], (PV, MISC)[k][:]).then_inc(s_oTs, 1)

        def dve_norm(dve, l, half):
            dve_stats(dve, l, half)
            dve_apply(dve, l, half)

        def dve_stats(dve, l, half):
            src = (xin, x)[l]
            for tt in (2 * half, 2 * half + 1):
                nc.vector.bn_stats(stats[:, tt, :], src[:, tt, :]).then_inc(s_stat[l], 1)
            dve.wait_ge(s_stat[l], 2 * half + 2)
            for tt in (2 * half, 2 * half + 1):
                nc.vector.bn_aggr(mv[:, tt, :], stats[:, tt, :]).then_inc(s_aggr[l], 1)

        def dve_apply(dve, l, half):
            src = (xin, x)[l]
            dve.wait_ge(s_rstd[l], half + 1)
            for tt in (2 * half, 2 * half + 1):
                last = nc.vector.tensor_scalar(xn[l][:, tt, :], src[:, tt, :], mv[:, tt, 0:1], rstd[:, tt:tt + 1],
                                               ALU.subtract, ALU.mult)
            last.then_inc(s_xn[l], 1)

        def pool_norm(pool, l, half):
            tts = slice(2 * half, 2 * half + 2)
            pool.wait_ge(s_aggr[l], 2 * half + 2)
            nc.gpsimd.tensor_scalar(rstd[:, tts], mv[:, tts, 1], EPS, None, ALU.add).then_inc(s_veps[l], 1)
            pool.wait_ge(s_veps[l], half + 1)
            nc.gpsimd.tensor_tensor(rstd[:, tts], rstd[:, tts], minus_half[:, 0:2], ALU.pow).then_inc(s_rstd[l], 1)

        def dve_turn(dve, l, half):
            for k in range(KC):
                dve.wait_ge(s_xnhi[l], 2 * half + k + 1)
                cols = slice(half * 256, half * 256 + 256)
                nc.vector.tensor_tensor(xnT[l][:, 1, k, cols], MX[k][:, cols], xnT[l][:, 0, k, cols].bitcast(F32),
                                        ALU.subtract).then_inc(s_xnlo[l], 1)

        def dve_project(dve, l, i):
            m = PROJ[l][i][2]
            bk = [[MX[0], MX[1], MX[0]], [SC[0], SC[1], MX[0], MX[1]]][l][i]
            dve.wait_ge(s_proj[l], i + 1)
            if l == 1:
                nc.vector.tensor_scalar(stage(i, 1)[0:m, :], bk[0:m, :], QK_MAX, -QK_MAX, ALU.min,
                                        ALU.max).then_inc(s_pc[1], 1)
            else:
                nc.vector.tensor_copy(stage(i, 1)[0:m, :], bk[0:m, :]).then_inc(s_pc[0], 1)

        def project_low(engine, eng, l, i):
            m = PROJ[l][i][2]
            eng.wait_ge(s_phi[l], i + 1)
            engine.tensor_tensor(stage(i, 1)[0:m, :].bitcast(F32R), stage(i, 1)[0:m, :], stage(i, 0)[0:m, :],
                                 ALU.subtract).then_inc(s_plo[l], 1)

        def dve_maxima(dve, u, i):
            qt, g0, heads = MAX_PACKS[i]
            w = P * (qt + 1)
            k, before = mx(u)
            n = PACKS * before + i
            dve.wait_ge(s_mp[k], n + 1)
            if i == 0 and before >= 2:
                dve.wait_ge(s_mT[1], before - 1)
            nc.vector.tensor_reduce(nmax[:, u % 2, g0:g0 + heads, qt],
                                    MX[n % 2][:, 0:heads * w].rearrange("p (g n) -> p g n", g=heads),
                                    AX.X, ALU.max, negate=True).then_inc(s_mr[k], 1)

        def dve_distances(dve, u, kt, g):
            w = T - P * kt
            dve.wait_ge(s_exp, PACKS * u + PACKS_TO[kt])
            if u:
                dve.wait_ge(s_es, u)
            pr = probs[:, kt % 2, g, 0:w]
            nc.vector.scalar_tensor_tensor(pr, pr, BIG, estrip[:, g, 0:w], ALU.min, ALU.mult).then_inc(s_pm, 1)

        def pool_distances(pool, u, kt):
            w = T - P * kt
            pool.wait_ge(s_exp, PACKS * u + PACKS_TO[kt])
            if u:
                pool.wait_ge(s_es, u)
            pr = probs[:, kt % 2, 2:4, :]
            nc.gpsimd.affine_select(pr[:, :, 0:P], pr[:, :, 0:P], [[0, 2], [1, P]], ALU.is_ge, 0.0, base=0,
                                    channel_multiplier=-1).then_inc(s_pc2, 1)
            pool.wait_ge(s_pc2, 4 * u + kt + 1)
            nc.gpsimd.tensor_tensor(pr[:, :, 0:w], pr[:, :, 0:w], estrip[:, 2:4, 0:w], ALU.mult).then_inc(s_pm2, 1)

        def dve_gate_half(dve, j):
            dve.wait_ge(s_t, j + 1 + (2 if j >= HT[0] else 0))
            nc.vector.scalar_tensor_tensor(hbuf[:, layer_tile(j)[1], :], tb[:], 1.0, FB[0][:], ALU.add,
                                           ALU.mult).then_inc(s_gu, 1)

        def dve_linear_half(dve, j):
            if j:
                dve.wait_ge(s_u, j)
            dve.wait_ge(s_gu, j + 1)
            h = hbuf[:, layer_tile(j)[1], :]
            nc.vector.scalar_tensor_tensor(h, h, 0.5, FB[1][:], ALU.mult, ALU.mult).then_inc(s_h, 1)

        def dve_down_half(dve, l, half):
            dve.wait_ge(s_t, (HT[0], J_ALL + 2)[l] + half + 1)
            nc.vector.scalar_tensor_tensor(fo[:, 2 * half:2 * half + 2, :].rearrange("p t c -> p (t c)"), tb[:], 1.0,
                                           FB[half][:], ALU.add, ALU.mult).then_inc(s_fo, 1)

        def dve_normalise(dve, u):
            l = layer_of(u)
            dve.wait_ge(s_oTp, u + 1)
            m = MISC[:].rearrange("p (a c) -> p a c", c=32)
            if u:
                dve.wait_ge(s_on, u)
            nc.vector.reciprocal(rden[:], m[:, :, DV]).then_inc(s_rd, 1)
            dve.wait_ge(s_rd, u + 1)
            if l == 0:
                o = o_sb[0][:, :, 64 * u:64 * u + 64].rearrange("p t (g d) -> p t g d", g=G4)
            else:
                w = u - U0[1]
                o = on[:, :, 4 * w:4 * w + 4, :]
            nc.vector.tensor_tensor(
                o, MISC[:].rearrange("p (t g c) -> p t g c", t=NT, g=G4)[:, :, :, 0:DV],
                rden[:].rearrange("p (t g) -> p t g", t=NT).unsqueeze(3).to_broadcast([P, NT, G4, DV]),
                ALU.mult).then_inc(s_on, 1)

        def dve_router(dve):
            sc, scb, top, two_, w, rep = (rt[:, i] for i in range(6))
            dve.wait_ge(s_rsg, 1)
            nc.vector.tensor_scalar(sc, sc, 1.0, 0.5, ALU.add, ALU.mult).then_inc(s_rtk, 1)
            dve.wait_ge(s_rtk, 1)
            nc.vector.tensor_tensor(scb, sc, bias_e[:].unsqueeze(1).to_broadcast([P, NT, NE]), ALU.add).then_inc(s_rtk, 1)
            dve.wait_ge(s_rtk, 2)
            for tt in range(NT):
                last = nc.vector.max(top[:, tt, :], scb[:, tt, :])
            last.then_inc(s_rtk, 1)
            dve.wait_ge(s_rtk, 3)
            nc.vector.tensor_copy(two_[:, :, 0:2], top[:, :, 0:2]).then_inc(s_rtk, 1)
            dve.wait_ge(s_rtk, 4)
            for tt in range(NT):
                last = nc.vector.match_replace(rep[:, tt, :], two_[:, tt, :], scb[:, tt, :], -BIG)
            last.then_inc(s_rtk, 1)
            dve.wait_ge(s_rtk, 5)
            nc.vector.scalar_tensor_tensor(w, rep, -BIG, sc, ALU.is_equal, ALU.mult).then_inc(s_rtk, 1)
            dve.wait_ge(s_rtk, 6)
            nc.vector.tensor_reduce(rs[:], w, AX.X, ALU.add).then_inc(s_rtk, 1)
            dve.wait_ge(s_rtk, 7)
            nc.vector.reciprocal(rs[:], rs[:]).then_inc(s_rtk, 1)
            dve.wait_ge(s_rtk, 8)
            nc.vector.tensor_tensor(w, w, rs[:].unsqueeze(2).to_broadcast([P, NT, NE]), ALU.mult).then_inc(s_rtk, 1)

        def dve_rms(dve):
            pair = on.rearrange("p t (h two) d -> p (t h) two d", two=2)
            o3 = o_sb[1][:].rearrange("p t (h d) -> p (t h) d", d=DV)
            sq = xn[0][:].rearrange("p t (h d) -> p (t h) d", d=DV)
            ms, y, a, sh = (nw[:, i, :] for i in range(4))
            n = 0

            def step(instruction):
                nonlocal n
                n += 1
                instruction.then_inc(s_rm, 1)
                dve.wait_ge(s_rm, n)

            dve.wait_ge(s_on, U_ALL)
            step(nc.vector.scalar_tensor_tensor(o3, pair[:, :, 1, :], lam[:, 5:6], pair[:, :, 0, :], ALU.mult, ALU.add))
            dve.wait_ge(s_xnTp[0], 2)
            step(nc.vector.tensor_tensor(sq, o3, o3, ALU.mult))
            step(nc.vector.tensor_reduce(ms, sq, AX.X, ALU.add))
            step(nc.vector.tensor_scalar(ms, ms, 1.0 / DV, EPS, ALU.mult, ALU.add))
            step(nc.vector.tensor_scalar(sh.bitcast(I32), ms.bitcast(I32), 1, None, ALU.arith_shift_right))
            step(nc.vector.tensor_scalar(y.bitcast(I32), sh.bitcast(I32), -1.0, RSQRT_MAGIC, ALU.mult, ALU.add))
            for _ in range(3):
                step(nc.vector.tensor_tensor(a, y, y, ALU.mult))
                step(nc.vector.scalar_tensor_tensor(a, a, -0.5, ms, ALU.mult, ALU.mult))
                step(nc.vector.scalar_tensor_tensor(y, a, 1.5, y, ALU.add, ALU.mult))
            step(nc.vector.tensor_tensor(o3, o3, y.unsqueeze(2).to_broadcast([P, 64, DV]), ALU.mult))
            nc.vector.tensor_tensor(o3, o3, gln[:].unsqueeze(1).to_broadcast([P, 64, DV]), ALU.mult).then_inc(s_rm, 1)
            assert n + 1 == RMS_STEPS

        def dve_update_x(dve, l, half):
            dve.wait_ge(s_so, 2 * l + half + 1)
            dve.wait_ge(s_fo, 2 * l + half + 1)
            tts = slice(2 * half, 2 * half + 2)
            f = fo[:, tts, :].rearrange("p t c -> p (t c)")
            nc.vector.scalar_tensor_tensor(f, SC[half][:], 0.5, f, ALU.mult, ALU.mult).then_inc(s_gx, 1)
            dve.wait_ge(s_gx, 2 * l + half + 1)
            nc.vector.tensor_tensor(x[:, tts, :], (xin, x)[l][:, tts, :], fo[:, tts, :], ALU.add).then_inc(s_xr, 1)
            dve.wait_ge(s_xr, 2 * l + half + 1)

        def act_up_high(act, t):
            s = t % n_ustage
            act.wait_ge(s_uin[s], 16 * (t // n_ustage + 1))
            nc.scalar.copy(hbuf[:, 2 * s, :].bitcast(F32R), hbuf[:, 2 * s + 1, :]).then_inc(s_uhi, 1)

        def dve_up_low(dve, t):
            s = t % n_ustage
            dve.wait_ge(s_uhi, t + 1)
            nc.vector.tensor_tensor(hbuf[:, 2 * s + 1, :].bitcast(F32R), hbuf[:, 2 * s + 1, :], hbuf[:, 2 * s, :],
                                    ALU.subtract).then_inc(s_ulo, 1)

        with nc.Block() as block:
            @block.sync
            def _(sp):
                load_x(sp, slice(0, T))
                small = ((ident[:], c_ident), (hadamard, c_hadamard), (causal_f, c_causal), (dist[:], c_dist),
                         (bias_e[:], gate_bias.partition_broadcast(P)),
                         (lam_in[:].rearrange("p a b -> p (a b)"), lambdas.partition_broadcast(P)),
                         (gln[:], subln.partition_broadcast(P)))
                for dst, src in small:
                    sp.dma_start(dst, src).then_inc(s_small, 16)
                for dst, _, src in raw:
                    sp.dma_start(dst, src.rearrange("p k n -> p (k n)")).then_inc(s_raw, 16)
                sp.dma_start(wdown[0][:], w0_down).then_inc(s_wd, 16)
                sp.wait_ge(s_zero, 1)
                sp.wait_ge(s_qz, 1)
                for s in (0, 1):
                    sp.dma_start(kring[0][MROW:MROW + 1, s, :].bitcast(F32), ones_row[0:1, :]).then_inc(s_kones, 16)
                write_images(sp, 0, range(3))
                ring_load(sp, 0)
                ring_load(sp, 1)
                for j in range(UP_SLOTS):
                    sp.wait_ge(s_uout[j], 16)
                    up_load(sp, j, s_uppre[j])
                max_row(sp, 0)
                wait_images(sp, 0, 3)
                sp.wait_ge(s_ring[1], 32)
                for j in range(UP_SLOTS):
                    sp.wait_ge(s_uppre[j], 16)
                sp.wait_ge(s_mrow[0], 16)
                sp.wait_ge(s_kones, 32)

            @block.gpsimd
            def _(pool):
                for t in range(n_ustage):
                    nc.gpsimd.dma_start(hbuf[:, 2 * t + 1, :], w_up[t]).then_inc(s_uin[t], 16)
                pool.wait_ge(s_zero, 1)
                for half in (0, 1):
                    pool_norm(pool, 0, half)
                nc.gpsimd.memset(qring[0][:].rearrange("p a g n -> p (a g n)").bitcast(F32), 0.0)
                nc.gpsimd.memset(kring[0][:].rearrange("p a n -> p (a n)").bitcast(F32), 0.0).then_inc(s_qz, 1)
                for t in range(J_ALL):
                    s = t % n_ustage
                    pool.wait_ge(s_uhi, t + 1)
                    pool.wait_ge(s_ulo, t + 1)
                    nc.gpsimd.dma_start(up_img[t], hbuf[:, 2 * s:2 * s + 2, :].rearrange("p a n -> p (a n)"))\
                        .then_inc(s_uout[s], 16)
                    if t >= 1 and t + n_ustage - 1 < J_ALL:
                        n = t + n_ustage - 1
                        pool.wait_ge(s_uout[n % n_ustage], 16 * (n // n_ustage))
                        nc.gpsimd.dma_start(hbuf[:, 2 * (n % n_ustage) + 1, :], w_up[n])\
                            .then_inc(s_uin[n % n_ustage], 16)
                    if t in (4, 5):
                        nc.gpsimd.dma_start((q_img, k_img)[t - 4][1][:, 24:32, :], zero_t).then_inc(s_pad, 16)
                    if t in (6, 8, 10):
                        dst, src = ((wo[0], w0_o), (wo[1], w1_o), (wdown[1], w1_down))[t // 2 - 3]
                        nc.gpsimd.dma_start(dst[:], src).then_inc(s_big, 16)
                pool.wait_ge(s_pad, 32)
                nc.gpsimd.dma_start(k_img[1][3:32:4, 31, :], ones_row[0:8, :]).then_inc(s_ones, 16)
                for s in range(n_ustage):
                    pool.wait_ge(s_uout[s], 16 * len(range(s, J_ALL, n_ustage)))
                pool.wait_ge(s_ones, 16)
                pool.wait_ge(s_big, 48)

            @block.tensor
            def _(pe):
                pe.wait_ge(s_small, 16 * 7)
                for half in (0, 1):
                    pe_turn(pe, 0, half)
                pe.wait_ge(s_xnlo[0], 2 * KC)
                pe.wait_ge(s_rlo, len(raw))
                for i in range(3):
                    pe_project(pe, 0, i)
                pe_v(pe, 0)
                wait_ring(pe, 0)
                pe.wait_ge(s_v[0], 1)
                pe.wait_ge(s_mask, 2)
                for i in range(PACKS):
                    pe_max_pack(pe, 0, i)
                pe_max_turn(pe, 0)
                pe.wait_ge(s_uppre[0], 16)
                for half in (0, 1):
                    pe_up_ahead(pe, half)
                nc.tensor.matmul(PV[:], zero_t[:, 0, 0:P], zero_t[:, 0, :], start=True, stop=True)
                pe.wait_ge(s_fw, 14)
                for t in range(HT[0]):
                    if t >= 2:
                        pe.wait_ge(s_hade, t - 1)
                    nc.tensor.matmul(SC[t % 2][:, 0:C], hadamard, tmp8[:, t, :], start=True, stop=True).then_inc(s_had, 1)

            @block.scalar
            def _(act):
                act.wait_ge(s_raw, 16 * len(raw))
                for stage_, w, _ in raw:
                    nc.scalar.copy(w[:, 0].rearrange("p k n -> p (k n)"), stage_).then_inc(s_rhi, 1)
                act_turn(act, 0, 0)
                act_up_high(act, 0)
                act_turn(act, 0, 1)
                act_up_high(act, 1)
                for i in range(3):
                    act_project(act, 0, i)
                    act_up_high(act, 2 + i)
                act.wait_ge(s_v0, 1)
                act_v(act, 0)
                act_strips(act, 0)
                for t in range(5, UP_EARLY):
                    act_up_high(act, t)
                act_max_copy(act, 0)
                for t in range(UP_EARLY, J_ALL):
                    act_up_high(act, t)
                    if t == UP_EARLY + 2:
                        act.wait_ge(s_lam, 3)
                        nc.scalar.activation(lam[:, 2:4], lam[:, 0:2], ACT.Exp).then_inc(s_lamx, 1)
                for t in range(HT[0]):
                    act.wait_ge(s_had, t + 1)
                    nc.scalar.copy(wdown[0][:, t, :], SC[t % 2][:, 0:C]).then_inc(s_hade, 1)

            @block.vector
            def _(dve):
                nc.vector.memset(zero_t, 0.0)
                nc.vector.memset(ones_row, 1.0)
                nc.vector.memset(minus_half[:], -0.5).then_inc(s_zero, 1)
                nc.vector.memset(v[0][:].rearrange("p t h d -> p (t h d)"), 1.0).then_inc(s_v0, 1)
                dve.wait_ge(s_x, 16)
                for half in (0, 1):
                    dve_norm(dve, 0, half)
                dve.wait_ge(s_raw, 16 * len(raw))
                for i, (stage_, w, _) in enumerate(raw):
                    dve.wait_ge(s_rhi, i + 1)
                    nc.vector.tensor_tensor(w[:, 1].rearrange("p k n -> p (k n)"), stage_,
                                            w[:, 0].rearrange("p k n -> p (k n)").bitcast(F32),
                                            ALU.subtract).then_inc(s_rlo, 1)
                dve_turn(dve, 0, 0)
                dve_up_low(dve, 0)
                dve_turn(dve, 0, 1)
                dve_up_low(dve, 1)
                for i in range(3):
                    dve_project(dve, 0, i)
                    project_low(nc.vector, dve, 0, i)
                    dve_up_low(dve, 2 + i)
                dve.wait_ge(s_small, 16 * 7)
                nc.vector.tensor_copy(ident_bf[:], ident[:]).then_inc(s_mask, 1)
                nc.vector.tensor_copy(causal_bf[:], causal_f.unsqueeze(1).to_broadcast([P, G4, P])).then_inc(s_mask, 1)
                for i in range(PACKS):
                    dve_maxima(dve, 0, i)
                    if i % 3 == 2:
                        dve_up_low(dve, 5 + i // 3)
                for t in range(UP_EARLY, J_ALL):
                    dve_up_low(dve, t)
                    if t == UP_EARLY:
                        for i in (0, 1):
                            nc.vector.tensor_tensor(lam_in[:, 2 * i, :], lam_in[:, 2 * i, :], lam_in[:, 2 * i + 1, :],
                                                    ALU.mult).then_inc(s_lam, 1)
                        dve.wait_ge(s_lam, 2)
                        nc.vector.tensor_reduce(lam[:, 0:2], lam_in[:, 0:4:2, :], AX.X, ALU.add).then_inc(s_lam, 1)
                    if t == UP_EARLY + 3:
                        dve.wait_ge(s_wd, 16)
                        src, dst = wdown[0][:], tmp8
                        n = 0
                        for b in (1, 2, 4):
                            for i in range(0, HT[0], 2 * b):
                                lo, hi = slice(i, i + b), slice(i + b, i + 2 * b)
                                nc.vector.tensor_tensor(dst[:, lo, :], src[:, lo, :], src[:, hi, :],
                                                        ALU.add).then_inc(s_fw, 1)
                                nc.vector.tensor_tensor(dst[:, hi, :], src[:, lo, :], src[:, hi, :],
                                                        ALU.subtract).then_inc(s_fw, 1)
                                n += 2
                            dve.wait_ge(s_fw, n)
                            src, dst = dst, src
                    if t == UP_EARLY + 6:
                        nc.vector.memset(qring[1][:].rearrange("p a g n -> p (a g n)").bitcast(F32), 0.0)
                    if t == UP_EARLY + 9:
                        nc.vector.memset(v[1][:].rearrange("p t h d -> p (t h d)"), 1.0)
                        nc.vector.memset(rt[:].rearrange("p a t e -> p (a t e)"), BIG)
                dve.wait_ge(s_lamx, 1)
                nc.vector.tensor_tensor(lam[:, 4:5], lam[:, 3:4], lam[:, 2:3], ALU.subtract).then_inc(s_lam, 1)
                dve.wait_ge(s_lam, 4)
                nc.vector.tensor_scalar(lam[:, 5:6], lam[:, 4:5], -LAMBDA_INIT, None, ALU.add)
                nc.vector.tensor_scalar(gln[:], gln[:], 1.0 - LAMBDA_INIT, None, ALU.mult)

        nc.gpsimd.dma_reset()
        nc.all_engine_barrier()
        clear(setup_sems + body_sems)
        nc.all_engine_barrier()

        with nc.Fori(0, B) as b:
            with nc.Block() as block:
                @block.sync
                def _(sp):
                    def rest_of_unit(u):
                        for j in (TILE_IN.get(u), TILE_AFTER.get(u)):
                            if j is not None and UP_SLOTS < j + 2 < J_ALL:
                                up_load(sp, j + 2)
                        if not last_of_layer(u) and not last_of_layer(u + 1):
                            sp.wait_ge(s_sc, PACKS * (u + 1))
                            ring_load(sp, u + 2)
                        if not last_of_layer(u):
                            max_row(sp, u + 1)

                    up_load(sp, UP_SLOTS)
                    for u in range(UNITS[0]):
                        rest_of_unit(u)
                    up_load(sp, FRONT_TILES[0] + 2)
                    write_images(sp, 1, (0, 1))
                    ring_load(sp, UNITS[0])
                    up_load(sp, FRONT_TILES[1] + 2)
                    ring_load(sp, UNITS[0] + 1)
                    up_load(sp, FRONT_TILES[2] + 2)
                    write_images(sp, 1, (2, 3))
                    for j in FRONT_TILES[3:-1]:
                        up_load(sp, j + 2)
                    max_row(sp, UNITS[0])
                    up_load(sp, FRONT_TILES[-1] + 2)
                    load_x(sp, bass.ds((b + 1) * T, T))
                    for u in range(UNITS[0], U_ALL):
                        rest_of_unit(u)
                    sp.wait_ge(s_u, J_ALL - 1)
                    for j in range(UP_SLOTS):
                        sp.dma_start(upring[:, j].rearrange("p a h k n -> p (a h k n)").bitcast(F32), up_img[j])\
                            .then_inc(s_uppre[j], 16)
                    write_images(sp, 0, range(3))
                    ring_load(sp, 0)
                    ring_load(sp, 1)
                    for half in (0, 1):
                        if half:
                            max_row(sp, 0)
                        sp.wait_ge(s_xr, 3 + half)
                        sp.dma_start(out[bass.ds(b * T + half * T // 2, T // 2), :].rearrange("(t p) c -> p t c", p=P),
                                     x[:, 2 * half:2 * half + 2, :]).then_inc(s_out, 16)
                    wait_images(sp, 0, 3)
                    sp.wait_ge(s_ring[1], 32)
                    for j in range(UP_SLOTS):
                        sp.wait_ge(s_uppre[j], 16)
                    sp.wait_ge(s_mrow[0], 16)
                    sp.wait_ge(s_out, 32)

                @block.tensor
                def _(pe):
                    def unit(u):
                        more = not last_of_layer(u)
                        if more:
                            wait_ring(pe, u + 1)
                        for i in range(PACKS):
                            pe_score_pack(pe, u, i)
                            if more:
                                pe_max_pack(pe, u + 1, i)
                            if more and u in TILE_IN:
                                pe_up_between(pe, TILE_IN[u], i)
                            if u == UNITS[0] - 1 and i < 8:
                                pe_up_between(pe, TILE_IN[u], i, 2, 8)
                            if u == U_ALL - 1 and i < UP_STEPS:
                                pe_up(pe, TILE_AFTER[u], 0, i, 1)
                            if i == 3 and u not in U0:
                                pe_out_turn(pe, u - 1)
                            if i == (7, 5)[layer_of(u)]:
                                pe_pv(pe, u, 0)
                            if u == U_ALL - 1 and i in (5, 8):
                                pe_turn(pe, 0, (5, 8).index(i))
                        pe_pv(pe, u, 1)
                        if more:
                            if u:
                                pe.wait_ge(s_on, u)
                            pe_max_turn(pe, u + 1)
                        if u < U_ALL - 1:
                            pe_up(pe, TILE_AFTER[u], 0)
                        pe_up(pe, TILE_AFTER[u], 1)
                        pe_pv(pe, u, 2)
                        pe_pv(pe, u, 3)
                    for u in range(UNITS[0]):
                        unit(u)
                    some, rest = range(HT[0] // 2), range(HT[0] // 2, HT[0])
                    pe_down(pe, 0, 0)
                    pe_out_turn(pe, UNITS[0] - 1)
                    pe_down(pe, 0, 1)
                    pe_o_turn(pe, 0)
                    pe_down(pe, 0, 2, some)
                    pe_attention_out(pe, 0, 0)
                    pe_down(pe, 0, 2, rest)
                    pe_attention_out(pe, 0, 1)
                    pe_down(pe, 0, 3, some)
                    pe_turn(pe, 1, 0)
                    pe_down(pe, 0, 3, rest)
                    pe.wait_ge(s_xnlo[1], KC)
                    pe_v(pe, 1, (0, 1))
                    pe_router(pe, (0, 1))
                    pe.wait_ge(s_gx, 1)
                    pe_project(pe, 1, 0, 0)
                    pe.wait_ge(s_gx, 2)
                    pe_project(pe, 1, 1, 0)
                    pe_up(pe, FRONT_TILES[0], 0, tokens=0)
                    pe_turn(pe, 1, 1)
                    pe_up(pe, FRONT_TILES[0], 1, tokens=0)
                    pe.wait_ge(s_xnlo[1], 2 * KC)
                    pe_project(pe, 1, 0, 1)
                    pe_project(pe, 1, 1, 1)
                    pe_router(pe, (2, 3))
                    pe_v(pe, 1, (2, 3))
                    pe_up(pe, FRONT_TILES[0], 0, tokens=1)
                    pe_up(pe, FRONT_TILES[0], 1, tokens=1)
                    pe_project(pe, 1, 2)
                    pe_up(pe, FRONT_TILES[1], 0)
                    pe.wait_ge(s_rsg, 1)
                    pe_project(pe, 1, 3)
                    pe_up(pe, FRONT_TILES[1], 1)
                    pe_up(pe, FRONT_TILES[2], 0)
                    pe.wait_ge(s_v[1], 1)
                    pe.wait_ge(s_rtk, 9)
                    for tt in range(NT):
                        last = nc.tensor.transpose(MISC[0:NE, tt * P:(tt + 1) * P], rt[:, 4, tt, :], ident[:])
                    last.then_inc(s_rT, 1)
                    pe_up(pe, FRONT_TILES[2], 1)
                    pe.wait_ge(s_pc[1], 4)
                    wait_ring(pe, UNITS[0])
                    for i in range(PACKS):
                        pe_max_pack(pe, UNITS[0], i)
                        if i:
                            pe_up_between(pe, FRONT_TILES[3], i - 1, 3, PACKS - 1)
                    pe.wait_ge(s_rTc, 1)
                    pe_max_turn(pe, UNITS[0])
                    pe_up(pe, FRONT_TILES[4], 1)
                    pe_up(pe, FRONT_TILES[5], 0)
                    pe_up(pe, FRONT_TILES[5], 1)
                    for u in range(UNITS[0], U_ALL):
                        unit(u)
                    pe.wait_ge(s_xnlo[0], 2 * KC)
                    for i in range(3):
                        pe_project(pe, 0, i)
                    pe_v(pe, 0)
                    pe_out_turn(pe, U_ALL - 1)
                    pe_down(pe, 1, 0)
                    pe_down(pe, 1, 1)
                    wait_ring(pe, 0)
                    pe.wait_ge(s_v[0], 1)
                    work = [(tt, j) for tt in (2, 3) for j in range(HT[1])]
                    done = 0
                    for i in range(PACKS):
                        pe_max_pack(pe, 0, i)
                        upto = min(len(work), len(work) * (i + 1) // (PACKS - 2))
                        for tt, j in work[done:upto]:
                            pe_down(pe, 1, tt, [j])
                        done = upto
                        if i == 1:
                            pe_o_turn(pe, 1)
                        if i == 3:
                            pe_attention_out(pe, 1, 0)
                        if i == 5:
                            pe_attention_out(pe, 1, 1)
                    pe.wait_ge(s_fo, 3)
                    pe.wait_ge(s_uppre[0], 16)
                    pe_up_ahead(pe, 0, 0, UP_STEPS // 2)
                    pe_max_turn(pe, 0)
                    pe_up_ahead(pe, 0, UP_STEPS // 2, UP_STEPS // 2)
                    pe.wait_ge(s_fo, 4)
                    pe_up_ahead(pe, 1)

                @block.scalar
                def _(act):
                    def unit(u):
                        for i in range(PACKS):
                            if i == PACKS - 1 and not last_of_layer(u):
                                act_max_copy(act, u + 1)
                            act_exps(act, u, i)
                            if i == 1 and u not in U0:
                                act_pv_copy(act, u - 1)
                            if i == 1 and u == 0:
                                act_tanh(act, 0)
                            if i == 6 and u in TILE_IN:
                                act_tanh(act, TILE_IN[u])
                            if u == U_ALL - 1 and i in (6, 9):
                                act_turn(act, 0, (6, 9).index(i))
                            if u == U_ALL - 1 and i == 7:
                                act_tanh(act, TILE_AFTER[u])
                        if u < U_ALL - 1:
                            act_tanh(act, TILE_AFTER[u])
                        if u < UNITS[0] - 1:
                            act.wait_ge(s_pm, 8 * u + 8)
                            act.wait_ge(s_pm2, 4 * u + 4)
                            act_strips(act, u + 1)
                        if last_of_layer(u):
                            act_pv_copy(act, u)

                    for u in range(UNITS[0]):
                        unit(u)
                    act_tanh_down(act, 0, 0)
                    act_o_turn(act, 0)
                    act_turn(act, 1, 0)
                    act_tanh_down(act, 0, 1)
                    act_turn(act, 1, 1)
                    act_project(act, 1, 0)
                    act_project(act, 1, 1)
                    act.wait_ge(s_rp, 1)
                    nc.scalar.activation(rt[:, 0].rearrange("p t e -> p (t e)"), MX[1][:, 0:NT * NE], ACT.Tanh,
                                         scale=0.5).then_inc(s_rsg, 1)
                    act_v(act, 1)
                    act_tanh(act, FRONT_TILES[0])
                    act_project(act, 1, 2)
                    act_tanh(act, FRONT_TILES[1])
                    act_project(act, 1, 3)
                    act_tanh(act, FRONT_TILES[2])
                    act.wait_ge(s_rT, 1)
                    nc.scalar.copy(gT[:], MISC[0:NE, :]).then_inc(s_rTc, 1)
                    act_tanh(act, FRONT_TILES[3])
                    act_max_copy(act, UNITS[0])
                    for j in FRONT_TILES[4:]:
                        act_tanh(act, j)
                    for u in range(UNITS[0], U_ALL):
                        unit(u)
                    for i in range(3):
                        act_project(act, 0, i)
                    act_v(act, 0)
                    act.wait_ge(s_rm, 1)
                    act_strips(act, 0)
                    act_tanh_down(act, 1, 0)
                    act_o_turn(act, 1)
                    act_tanh_down(act, 1, 1)
                    act.wait_ge(s_mrow[1], 16 * (U_ALL - 1))
                    act_max_copy(act, 0)

                @block.vector
                def _(dve):
                    def unit(u):
                        more = not last_of_layer(u)
                        for i in range(PACKS):
                            if more:
                                dve_maxima(dve, u + 1, i)
                            if layer_of(u) == 0 and i in (4, 5, 8, 9):
                                dve_distances(dve, u, (4, 8).index(i // 4 * 4), i % 2)
                            if i == (6, 4)[layer_of(u)] and u not in U0:
                                dve_normalise(dve, u - 1)
                            if i == 1 and u == 0:
                                dve_gate_half(dve, 0)
                            if i == 2 and u == 0:
                                dve_linear_half(dve, 0)
                            if u in TILE_IN and i == 7:
                                dve_gate_half(dve, TILE_IN[u])
                        if u in TILE_IN:
                            dve_linear_half(dve, TILE_IN[u])
                        if layer_of(u) == 0:
                            for kt in (2, 3):
                                for g in (0, 1):
                                    dve_distances(dve, u, kt, g)
                        dve_gate_half(dve, TILE_AFTER[u])
                        dve_linear_half(dve, TILE_AFTER[u])
                        if last_of_layer(u) and u < U_ALL - 1:
                            dve_normalise(dve, u)

                    for u in range(UNITS[0]):
                        unit(u)
                    dve_down_half(dve, 0, 0)
                    dve_update_x(dve, 0, 0)
                    dve_norm(dve, 1, 0)
                    dve_turn(dve, 1, 0)
                    dve_down_half(dve, 0, 1)
                    dve_update_x(dve, 0, 1)
                    dve_norm(dve, 1, 1)
                    dve_turn(dve, 1, 1)
                    dve_project(dve, 1, 0)
                    dve_project(dve, 1, 1)
                    project_low(nc.vector, dve, 1, 0)
                    project_low(nc.vector, dve, 1, 1)
                    dve_router(dve)
                    dve_gate_half(dve, FRONT_TILES[0])
                    dve_linear_half(dve, FRONT_TILES[0])
                    dve_project(dve, 1, 2)
                    dve_gate_half(dve, FRONT_TILES[1])
                    dve_project(dve, 1, 3)
                    dve_linear_half(dve, FRONT_TILES[1])
                    dve_gate_half(dve, FRONT_TILES[2])
                    dve_linear_half(dve, FRONT_TILES[2])
                    for i in range(PACKS):
                        dve_maxima(dve, UNITS[0], i)
                        if i == 5:
                            dve_gate_half(dve, FRONT_TILES[3])
                        if i == 9:
                            dve_linear_half(dve, FRONT_TILES[3])
                    for j in FRONT_TILES[4:]:
                        dve_gate_half(dve, j)
                        dve_linear_half(dve, j)
                    for u in range(UNITS[0], U_ALL - 1):
                        unit(u)
                    dve.wait_ge(s_x, 16)
                    for half in (0, 1):
                        dve_stats(dve, 0, half)
                    dve_normalise(dve, U_ALL - 2)
                    for half in (0, 1):
                        dve_apply(dve, 0, half)
                    dve_turn(dve, 0, 0)
                    dve_gate_half(dve, TILE_AFTER[U_ALL - 1])
                    dve_turn(dve, 0, 1)
                    dve_linear_half(dve, TILE_AFTER[U_ALL - 1])
                    for i in range(3):
                        dve_project(dve, 0, i)
                    dve_normalise(dve, U_ALL - 1)
                    dve_rms(dve)
                    dve_down_half(dve, 1, 0)
                    dve.wait_ge(s_mT[1], U_ALL - 2)
                    for i in range(PACKS):
                        dve_maxima(dve, 0, i)
                        if i == 6:
                            dve_update_x(dve, 1, 0)
                        if i == PACKS - 2:
                            dve_down_half(dve, 1, 1)
                    dve_update_x(dve, 1, 1)

                def weigh(pool, j):
                    n = j - HT[0] - SHARED_T
                    if n < 0:
                        return
                    pool.wait_ge(s_h, j + 1)
                    pool.wait_ge(s_gr[n % 2], 16 * sum(len(gate_segments(m)) for m in range(n % 2, n + 1, 2)))
                    h = hbuf[:, j - HT[0], :]
                    nc.gpsimd.tensor_tensor(h, h, gring[:, n % 2, :], ALU.mult).then_inc(s_hw, 1)

                def gate_load(pool, j):
                    n = j - HT[0] - SHARED_T
                    if n < 0 or j >= J_ALL:
                        return
                    if n >= 2:
                        pool.wait_ge(s_hw, n - 1)
                    for e, r, m in gate_segments(n):
                        nc.gpsimd.dma_start(gring[r:r + m, n % 2, :],
                                            gate_img[e].partition_broadcast(m)).then_inc(s_gr[n % 2], 16)

                @block.gpsimd
                def _(pool):
                    for u in range(UNITS[0]):
                        for kt in range(NT):
                            pool_distances(pool, u, kt)
                    for half in (0, 1):
                        pool_norm(pool, 1, half)
                    pool.wait_ge(s_plo[1], 2)
                    for i in (2, 3):
                        project_low(nc.gpsimd, pool, 1, i)
                    pool.wait_ge(s_rTc, 1)
                    nc.gpsimd.dma_start(gate_img, gT[:]).then_inc(s_rimg, 16)
                    pool.wait_ge(s_rimg, 16)
                    first = HT[0] + SHARED_T
                    gate_load(pool, first)
                    gate_load(pool, first + 1)
                    for j in FRONT_TILES[:-2]:
                        if j >= first:
                            weigh(pool, j)
                            gate_load(pool, j + 2)
                    for u in range(UNITS[0], U_ALL):
                        if u == U_ALL - 1:
                            for half in (0, 1):
                                pool_norm(pool, 0, half)
                        for kt in range(NT):
                            pool.wait_ge(s_exp, PACKS * u + PACKS_TO[kt])
                            pr = probs[:, kt % 2, :, 0:P]
                            nc.gpsimd.affine_select(pr, pr, [[0, G4], [1, P]], ALU.is_ge, 0.0, base=0,
                                                    channel_multiplier=-1).then_inc(s_pm, 1)
                            if u == UNITS[0] and kt < 2:
                                weigh(pool, FRONT_TILES[kt - 2])
                                gate_load(pool, FRONT_TILES[kt - 2] + 2)
                            if u > UNITS[0] and kt == 0:
                                weigh(pool, TILE_AFTER[u - 1])
                                gate_load(pool, TILE_AFTER[u - 1] + 2)
                    weigh(pool, TILE_AFTER[U_ALL - 1])
                    for i in range(3):
                        project_low(nc.gpsimd, pool, 0, i)

            nc.gpsimd.dma_reset()
            nc.all_engine_barrier()
            clear(body_sems)
            nc.all_engine_barrier()


def kernel(**inputs):
    import numpy as np
    import concourse.bacc as bacc
    from concourse.bass_utils import run_bass_kernel_spmd

    a = {k: np.asarray(v) for k, v in inputs.items()}

    def chunks(w):
        return np.ascontiguousarray(w.T.reshape(KC, P, -1).transpose(1, 0, 2))

    def up_tiles(gate, lin):
        both = np.stack([gate, lin]).reshape(2, -1, P, KC, P)
        return both.transpose(1, 4, 0, 3, 2).reshape(-1, P, 2 * KC * P)

    def down_tiles(w):
        return np.ascontiguousarray(w.T.reshape(-1, P, C).transpose(1, 0, 2))

    hs = 352
    pad = np.zeros((SHARED_T * P - hs, C), np.float32)
    gw, up, dn = a["L1_ffn_shared_gw"], a["L1_ffn_up_w"], a["L1_ffn_down_w"]
    gate1 = np.concatenate([gw[hs:], pad, up[:, :EH].reshape(-1, C)])
    lin1 = np.concatenate([gw[:hs], pad, up[:, EH:].reshape(-1, C)])
    down1 = np.concatenate([a["L1_ffn_shared_dw"], pad.T, dn.transpose(1, 0, 2).reshape(C, -1)], axis=1)

    had = np.ones((1, 1), np.float32)
    while had.shape[0] < P:
        had = np.block([[had, had], [had, -had]])
    d = np.arange(T)[None, :] - np.arange(P)[:, None]
    dist = np.where(d >= 0, np.sqrt(np.maximum(d, 0)), 1.0e30).astype(np.float32)
    causal = np.where(np.arange(P)[None, :] <= np.arange(P)[:, None], 0.0, -BIG).astype(np.float32)
    xs = a["L0_attn_x"]
    arrays = {
        "x": np.concatenate([xs, xs[-1:]]).reshape(-1, C),
        "w0_qk": chunks(np.concatenate([a["L0_attn_Wq"], a["L0_attn_Wk"]])),
        "w0_v": chunks(a["L0_attn_Wv"]),
        "w0_o": chunks(a["L0_attn_Wo"]),
        "w_up": np.concatenate([up_tiles(a["L0_ffn_W1"], a["L0_ffn_W3"]), up_tiles(gate1, lin1)]),
        "w0_down": down_tiles(a["L0_ffn_W2"]),
        "w1_qk": chunks(np.concatenate([a["L1_attn_Wq"], a["L1_attn_Wk"]])),
        "w1_v": chunks(a["L1_attn_Wv"]),
        "w1_o": chunks(a["L1_attn_Wo"]),
        "w1_down": down_tiles(down1),
        "w1_gate": chunks(a["L1_ffn_gate_w"]),
        "gate_bias": a["L1_ffn_gate_bias"],
        "lambdas": np.concatenate([a[f"L1_attn_lambda_{n}"] for n in ("q1", "k1", "q2", "k2")]),
        "subln": a["L1_attn_subln_weight"],
        "c_ident": np.eye(P, dtype=np.float32),
        "c_hadamard": (had / 32).astype(np.float32),
        "c_dist": dist,
        "c_causal": causal,
    }
    nc = bacc.Bacc("TRN2", target_bir_lowering=False, num_devices=1)
    args = [nc.dram_tensor("in_" + n, v.shape, mybir.dt.from_np(v.dtype), kind="ExternalInput").ap()
            for n, v in arrays.items()]
    out = nc.dram_tensor("out", (B * T, C), F32, kind="ExternalOutput").ap()
    gated_layers_kernel(nc, *args, out)
    r = run_bass_kernel_spmd(nc, [{"in_" + n: v for n, v in arrays.items()}], core_ids=[0])
    return r.results[0]["out"].reshape(B, T, C)
```
